# Optimizing a Trainium2 kernel written in Bass

```python
import numpy as np
import jax
import jax.numpy as jnp

def _softmax(x, axis=-1):
    return jax.nn.softmax(x, axis=axis)

def _gelu(x):
    return jax.nn.gelu(x, approximate=True)

def _silu(x):
    return jax.nn.silu(x)

def _sigmoid(x):
    return jax.nn.sigmoid(x)

def _layernorm(x, axis=-1, eps=1e-05):
    m = jnp.mean(x, axis=axis, keepdims=True)
    v = jnp.var(x, axis=axis, keepdims=True)
    return (x - m) / jnp.sqrt(v + eps)

def _scatter_add(tgt, idx, src, axis=0):
    return tgt.at[idx].add(src)

def _segment_sum(src, seg, n):
    return jax.ops.segment_sum(src, seg, n)
kernel_name = 'mk_adaln_ffn_d1_seqx_r8_1d7a0b'

def setup_inputs(seed: int=0):
    np.random.seed(seed)
    _w = jnp.asarray

    def _rec_inputs():
        import jax
        import jax.numpy as jnp
        _rk = jax.random.key(seed)
        x = 7.22e-05 + 1 * jax.random.normal(jax.random.fold_in(_rk, 1), (8, 128, 256), jnp.float32)
        _lenS = 128 - jax.random.randint(jax.random.fold_in(_rk, 7), (8,), 0, max(1, 128 // 4) + 1, jnp.int32)
        _lenS2 = 128 - jax.random.randint(jax.random.fold_in(_rk, 8), (8,), 0, max(1, 128 // 4) + 1, jnp.int32)
        cond_2048 = jax.random.bernoulli(jax.random.fold_in(_rk, 11), 0.5063, (8, 256)).astype(jnp.float32)
        return (x, cond_2048)
    x, cond_2048 = _rec_inputs()

    def _L0_cond_setup():
        import jax, jax.numpy as jnp
        import numpy as np
        NH = 8
        NEG = -1e+30
        key = jax.random.key(seed)
        k1, k2, k3, k4 = jax.random.split(key, 4)
        B, D, T = (4, 128, 256)
        x = jax.random.normal(k1, (B, D, T), dtype=jnp.float32)
        mask = jax.random.randint(k2, (B, T), 0, 2).astype(jnp.float32)
        lim = float(np.sqrt(6.0 / (D + D)))
        Wq = jax.random.uniform(k3, (D, D), dtype=jnp.float32, minval=-lim, maxval=lim)
        Wo = jax.random.uniform(k4, (D, D), dtype=jnp.float32, minval=-lim, maxval=lim)
        return {'x': x, 'mask': mask, 'Wq': Wq, 'Wo': Wo}
    _L0_cond_all = _L0_cond_setup()
    _L0_cond_in = {k: v for k, v in _L0_cond_all.items() if k in ('Wq', 'Wo')}
    del _L0_cond_all

    def _L0_ffn_setup():
        import jax, jax.numpy as jnp
        import numpy as np
        from jax import lax
        DIM = 256
        INTER = 176
        N_EXPERTS = 32
        TOP_K = 6
        N_SHARED = 2
        CAPACITY = 256
        ROUTE_SCALE = 1.0

        def _gate(xf, gate_w):
            logits = xf @ gate_w.T
            scores = jax.nn.softmax(logits.astype(jnp.float32), axis=-1)
            top_w, top_i = lax.top_k(scores, TOP_K)
            return ((top_w * ROUTE_SCALE).astype(xf.dtype), top_i)

        def _moe(xf, gate_w, w1, w2, w3):
            T, D = xf.shape
            E, CAP = (N_EXPERTS, CAPACITY)
            top_w, top_i = _gate(xf, gate_w)
            e_flat = top_i.reshape(-1)
            t_flat = jnp.repeat(jnp.arange(T), TOP_K)
            w_flat = top_w.reshape(-1)
            order = jnp.argsort(e_flat)
            e_s, t_s, w_s = (e_flat[order], t_flat[order], w_flat[order])
            counts = jnp.zeros((E,), jnp.int32).at[e_s].add(1)
            starts = jnp.concatenate([jnp.zeros((1,), jnp.int32), jnp.cumsum(counts)[:-1]])
            pos = jnp.arange(T * TOP_K, dtype=jnp.int32) - starts[e_s]
            valid = pos < CAP
            buf_idx = jnp.where(valid, e_s * CAP + pos, E * CAP)
            xbuf = jnp.zeros((E * CAP + 1, D), xf.dtype).at[buf_idx].set(xf[t_s])
            xb = xbuf[:E * CAP].reshape(E, CAP, D)
            h = jax.nn.silu(jnp.einsum('ecd,edi->eci', xb, w1)) * jnp.einsum('ecd,edi->eci', xb, w3)
            ob = jnp.einsum('eci,eid->ecd', h, w2).reshape(E * CAP, D)
            ob = jnp.concatenate([ob, jnp.zeros((1, D), ob.dtype)], axis=0)
            y_pairs = ob[buf_idx] * w_s[:, None]
            y = jnp.zeros((T, D), xf.dtype).at[t_s].add(y_pairs)
            return y
        key = jax.random.key(seed)
        ks = jax.random.split(key, 9)
        B, S = (4, 256)
        si = INTER * N_SHARED
        inputs = {'x': jax.random.normal(ks[0], (B, S, DIM), jnp.float32), 'gate_w': jax.random.normal(ks[1], (N_EXPERTS, DIM), jnp.float32), 'w1': jax.random.normal(ks[2], (N_EXPERTS, DIM, INTER), jnp.float32) * DIM ** (-0.5), 'w2': jax.random.normal(ks[3], (N_EXPERTS, INTER, DIM), jnp.float32) * INTER ** (-0.5), 'w3': jax.random.normal(ks[4], (N_EXPERTS, DIM, INTER), jnp.float32) * DIM ** (-0.5), 'sw1': jax.random.normal(ks[5], (DIM, si), jnp.float32) * DIM ** (-0.5), 'sw2': jax.random.normal(ks[6], (si, DIM), jnp.float32) * si ** (-0.5), 'sw3': jax.random.normal(ks[7], (DIM, si), jnp.float32) * DIM ** (-0.5)}
        return inputs
    _L0_ffn_all = _L0_ffn_setup()
    _L0_ffn_in = {k: v for k, v in _L0_ffn_all.items() if k in ('gate_w', 'w1', 'w2', 'w3', 'sw1', 'sw2', 'sw3')}
    del _L0_ffn_all
    return {'x': x, 'cond_2048': cond_2048, 'L0_cond_Wq': _L0_cond_in['Wq'], 'L0_cond_Wo': _L0_cond_in['Wo'], 'L0_ffn_gate_w': _L0_ffn_in['gate_w'], 'L0_ffn_w1': _L0_ffn_in['w1'], 'L0_ffn_w2': _L0_ffn_in['w2'], 'L0_ffn_w3': _L0_ffn_in['w3'], 'L0_ffn_sw1': _L0_ffn_in['sw1'], 'L0_ffn_sw2': _L0_ffn_in['sw2'], 'L0_ffn_sw3': _L0_ffn_in['sw3']}

def reference(x, cond_2048, L0_cond_Wq, L0_cond_Wo, L0_ffn_gate_w, L0_ffn_w1, L0_ffn_w2, L0_ffn_w3, L0_ffn_sw1, L0_ffn_sw2, L0_ffn_sw3):
    import jax
    import jax.numpy as jnp

    def _L0_cond_ref(x, mask, Wq, Wo):
        import jax, jax.numpy as jnp
        import numpy as np
        NH = 8
        NEG = -1e+30
        B, D, T = x.shape
        dk = D // NH
        scale = 1.0 / jnp.sqrt(jnp.asarray(dk, x.dtype))
        xt = jnp.transpose(x, (0, 2, 1))
        q = xt @ Wq.T
        qh = q.reshape(B, T, NH, dk).transpose(0, 2, 1, 3)
        scores = scale * jnp.einsum('bhqd,bhkd->bhqk', qh, qh)
        cmask = mask[:, None, None, :]
        rmask = mask[:, None, :, None]
        logits = (scores * cmask + (1.0 - cmask) * NEG) * rmask
        attn = jax.nn.softmax(logits, axis=-1)
        ctx = jnp.einsum('bhqk,bhkd->bhqd', attn, qh)
        ctx = ctx.transpose(0, 2, 1, 3).reshape(B, T, D)
        out = ctx @ Wo.T
        return jnp.transpose(out, (0, 2, 1))

    def _L0_ffn_ref(x, gate_w, w1, w2, w3, sw1, sw2, sw3):
        import jax, jax.numpy as jnp
        import numpy as np
        from jax import lax
        DIM = 256
        INTER = 176
        N_EXPERTS = 32
        TOP_K = 6
        N_SHARED = 2
        CAPACITY = 256
        ROUTE_SCALE = 1.0

        def _gate(xf, gate_w):
            logits = xf @ gate_w.T
            scores = jax.nn.softmax(logits.astype(jnp.float32), axis=-1)
            top_w, top_i = lax.top_k(scores, TOP_K)
            return ((top_w * ROUTE_SCALE).astype(xf.dtype), top_i)

        def _moe(xf, gate_w, w1, w2, w3):
            T, D = xf.shape
            E, CAP = (N_EXPERTS, CAPACITY)
            top_w, top_i = _gate(xf, gate_w)
            e_flat = top_i.reshape(-1)
            t_flat = jnp.repeat(jnp.arange(T), TOP_K)
            w_flat = top_w.reshape(-1)
            order = jnp.argsort(e_flat)
            e_s, t_s, w_s = (e_flat[order], t_flat[order], w_flat[order])
            counts = jnp.zeros((E,), jnp.int32).at[e_s].add(1)
            starts = jnp.concatenate([jnp.zeros((1,), jnp.int32), jnp.cumsum(counts)[:-1]])
            pos = jnp.arange(T * TOP_K, dtype=jnp.int32) - starts[e_s]
            valid = pos < CAP
            buf_idx = jnp.where(valid, e_s * CAP + pos, E * CAP)
            xbuf = jnp.zeros((E * CAP + 1, D), xf.dtype).at[buf_idx].set(xf[t_s])
            xb = xbuf[:E * CAP].reshape(E, CAP, D)
            h = jax.nn.silu(jnp.einsum('ecd,edi->eci', xb, w1)) * jnp.einsum('ecd,edi->eci', xb, w3)
            ob = jnp.einsum('eci,eid->ecd', h, w2).reshape(E * CAP, D)
            ob = jnp.concatenate([ob, jnp.zeros((1, D), ob.dtype)], axis=0)
            y_pairs = ob[buf_idx] * w_s[:, None]
            y = jnp.zeros((T, D), xf.dtype).at[t_s].add(y_pairs)
            return y
        shape = x.shape
        xf = x.reshape(-1, DIM)
        y = _moe(xf, gate_w, w1, w2, w3)
        shared = jax.nn.silu(xf @ sw1) * (xf @ sw3) @ sw2
        return (y + shared).reshape(shape)
    x = x + _L0_ffn_ref(_L0_cond_ref(x, cond_2048, L0_cond_Wq, L0_cond_Wo), L0_ffn_gate_w, L0_ffn_w1, L0_ffn_w2, L0_ffn_w3, L0_ffn_sw1, L0_ffn_sw2, L0_ffn_sw3)
    return x

_drawn_inputs = setup_inputs


def setup_inputs(seed=0):
    import zlib

    import numpy as np

    out = dict(_drawn_inputs(seed))
    spreads = {}
    factors = {}
    for name, (base, spread) in spreads.items():
        noise = np.random.default_rng([zlib.crc32(name.encode()), seed]).standard_normal(out[name].shape)
        drawn = base * np.exp(spread * noise) if base else spread * noise
        out[name] = jnp.asarray(drawn.astype(out[name].dtype))
    for name, factor in factors.items():
        out[name] = (out[name] * factor).astype(out[name].dtype)
    return out
```

```python
from contextlib import ExitStack

import concourse.bass as bass
from concourse import mybir

F32 = mybir.dt.float32
F32R = mybir.dt.float32r
I32 = mybir.dt.int32
U32 = mybir.dt.uint32
ALU = mybir.AluOpType
ACT = mybir.ActivationFunctionType
AX = mybir.AxisListType

P = 128
NB, D, T = 8, 128, 256
NH, DK = 8, 16
E, TOPK, CAP = 32, 6, 256
INTER, SI = 176, 352
TOK = NB * D
STEPS = NB * NH // 2
ROW = T + E + 1
TRASH = E * CAP
YROWS = TOK + CAP
HEADW = 112

C_ID, C_UP, C_DEN = 0, 128, 256
C_SEL = 384
C_IOTA = C_SEL + 256
C_SPLIT = C_IOTA + E
C_TRASH = C_SPLIT + 2
NCONST = C_TRASH + 1


def wait_apart(engine, signal, value, met, met_value):
    if not isinstance(value, int):
        register = engine.alloc_register()
        engine.reg_add(register, value, 0)
        value = register
    engine.wait_ge(met, met_value)
    engine.wait_ge(signal, value)


def build(nc, x, cond, wq, wo, gate_w, w1, w2, w3, sw1, sw2, sw3, cst, csti, out):
    ctx = ExitStack()
    with ctx:
        def sb(name, shape, dt=F32):
            return ctx.enter_context(nc.sbuf_tensor(name, shape, dt))

        def sem(name):
            return ctx.enter_context(nc.semaphore(name))

        rows_dram = nc.dram_tensor("expert_rows", [TRASH + P, ROW], F32).ap()
        y_dram = [nc.dram_tensor(f"y{i}", [YROWS, T], F32).ap() for i in range(2)]

        ps = ctx.enter_context(nc.psum_tensor("ps", [P, 8, 512], F32))

        X = sb("X", [P, NB, T])
        XFT = sb("XFT", [P, 2, TOK])
        SW13 = sb("SW13", [P, 2, 2, SI])
        SW2 = sb("SW2", [P, 3, T])
        RING = 4
        TAIL = INTER - HEADW
        W1 = [sb(f"W1_{i}", [P, 2, INTER + TAIL]) for i in range(RING)]
        W3 = [sb(f"W3_{i}", [P, 2, INTER]) for i in range(RING)]
        W2A = [sb(f"W2A_{i}", [HEADW, T]) for i in range(RING)]
        W2B = [sb(f"W2B_{i}", [INTER - HEADW, T]) for i in range(RING)]
        C = sb("C", [P, NCONST])
        CI = sb("CI", [P, NB + 2], I32)
        IDENT = C[:, C_ID:C_ID + P]
        ZERO = sb("ZERO", [P, T])
        FILL = sb("FILL", [P, 2, ROW])

        s_w = sem("shared_weights_loaded")
        s_ew = [sem(f"expert_weights_loaded{i}") for i in range(RING)]
        s_yzero = sem("y_zeroed")

        def load_expert(sp, e, m):
            w3e = w3[e].rearrange("(k p) n -> p k n", p=P)
            sp.dma_start(W1[m][:, :, 0:INTER], w1[e].rearrange("(k p) n -> p k n", p=P)).then_inc(s_ew[m], 16)
            sp.dma_start(W1[m][:, :, INTER:INTER + TAIL], w3e[:, :, HEADW:INTER]).then_inc(s_ew[m], 16)
            sp.dma_start(W3[m][:], w3e).then_inc(s_ew[m], 16)
            sp.dma_start(W2A[m][:], w2[e, 0:HEADW, :]).then_inc(s_ew[m], 16)
            sp.dma_start(W2B[m][:], w2[e, HEADW:INTER, :]).then_inc(s_ew[m], 16)

        attention(nc, sb, sem, ps, x, cond, wq, wo, gate_w, sw1, sw2, sw3, cst, csti,
                  rows_dram, y_dram, X, XFT, SW13, SW2, C, CI, IDENT, ZERO, FILL, s_w, s_yzero, load_expert)
        experts(nc, sb, sem, ps, rows_dram, y_dram, X, XFT, SW13, SW2, W1, W3, W2A, W2B, C, CI, IDENT,
                s_w, s_ew, s_yzero, load_expert, out)


def attention(nc, sb, sem, ps, x, cond, wq, wo, gate_w, sw1, sw2, sw3, cst, csti,
              rows_dram, y_dram, X, XFT, SW13, SW2, C, CI, IDENT, ZERO, FILL, s_w, s_yzero, load_expert):
    with ExitStack() as ctx:
        def sb(name, shape, dt=F32):
            return ctx.enter_context(nc.sbuf_tensor(name, shape, dt))

        MASKB = sb("MASKB", [P, NB, T])
        INV = sb("INV", [P, NB, T])
        XM = sb("XM", [P, NB, T])
        XI = sb("XI", [P, NB, T])
        XV = sb("XV", [P, T])
        COND = sb("COND", [NB, T])
        WQ = sb("WQ", [P, D])
        WO = sb("WO", [P, D])
        WOP = sb("WOP", [P, 2, 4, 32])
        WOT = sb("WOT", [P, 2, P])
        GW = sb("GW", [E, T])
        GWT = sb("GWT", [P, 2, E])
        MASKT = sb("MASKT", [P, 2, NB])
        WQT = sb("WQT", [P, D])
        WQR = sb("WQR", [P, 4, 2, 4, DK])
        WQG = sb("WQG", [P, 2, 4, 32])
        SEL = sb("SEL", [4, 2, P], F32R)
        XS = sb("XS", [P, 2, NB])
        SV = sb("SV", [P, 2, NB])
        HI = sb("HI", [P, 2, T], F32R)
        QA = sb("QA", [P, 4, T], F32R)
        QB = sb("QB", [P, 4, T], F32R)
        VP = sb("VP", [P, 2, NH, 32])
        EX = sb("EX", [P, 2, 2, 2, T])
        NEGMAX = sb("NEGMAX", [P, 2, 2])
        NM2 = sb("NM2", [P, 2, 2, 2])
        NMT = sb("NMT", [4, T], F32R)
        U = sb("U", [P, 2, T])
        DEN = sb("DEN", [P, 2, T])
        CT = sb("CT", [P, 2, T])
        PAY = sb("PAY", [P, ROW])
        YT = sb("YT", [P, 2, P])
        LG = sb("LG", [P, E])
        TOP = sb("TOP", [P, 8])
        TOPI = sb("TOPI", [P, 8], U32)
        TOPF = sb("TOPF", [P, 8])
        NTOP = sb("NTOP", [P, 1])
        ESUM = sb("ESUM", [P, 1])
        RSUM = sb("RSUM", [P, 1])
        ES = sb("ES", [P, E])
        ONEH = sb("ONEH", [P, TOPK, E])
        PICK = sb("PICK", [P, TOPK, E])
        CHOSEN = sb("CHOSEN", [P, E])
        BEFORE = sb("BEFORE", [P, E])
        ONES = sb("ONES", [P, P])
        PLACE = sb("PLACE", [P, TOPK])
        FITS = sb("FITS", [P, TOPK])
        SLOTF = sb("SLOTF", [P, TOPK])
        SLOT = sb("SLOT", [P, TOPK], I32)

        s_wload = sem("wq_wo_gate_consts_loaded")
        s_x0 = sem("x_loaded")
        s_mask = sem("mask_loaded")
        s_rowfill = sem("rows_filled")
        s_pre = sem("pool_prepared")
        s_wop = sem("wo_padded")
        s_tset = sem("setup_transposed")
        s_eset = sem("setup_copied")
        s_wqr = sem("wq_spread")
        s_xm = sem("x_masked")
        s_xs = sem("x_summed")
        s_svp = sem("masked_v_summed")
        s_sv = sem("masked_v_copied")
        s_pj = sem("projected")
        s_hi = sem("high_part_ready")
        s_ab = sem("q_operands_ready")
        s_xv = sem("xv_ready")
        s_ve = sem("v_ready")
        s_vo = sem("v_ones_ready")
        s_sc = sem("scores_ready")
        s_nm = sem("negmax_ready")
        s_nt = sem("negmax_transposed")
        s_nc = sem("negmax_copied")
        s_sh = sem("scores_shifted")
        s_ex = sem("exp_ready")
        s_pv = sem("pv_ready")
        s_u = sem("pv_copied")
        s_ct = sem("context_ready")
        s_wo = sem("out_projected")
        s_y = sem("y_copied")
        s_yt = sem("y_transposed")
        s_ytc = sem("yt_copied")
        s_xft = sem("xft_stored")
        s_lg = sem("logits_ready")
        s_top = sem("top_found")
        s_es = sem("router_exp_ready")
        s_ch = sem("choices_ready")
        s_ct2 = sem("choices_counted")
        s_slot = sem("slots_ready")
        s_scat = sem("rows_scattered")
        s_dve = sem("vector_in_order")
        s_pool = sem("pool_in_order")

        B_PO, B_PJ, B_NM, B_FIN = 4, 5, 6, 7

        def scores(t2):
            return ps[:, 2 * t2:2 * t2 + 2, :]

        block = ctx.enter_context(nc.Block())

        @block.sync
        def _(sp):
            sp.dma_start(WQ[:], wq).then_inc(s_wload, 16)
            sp.dma_start(C[:], cst).then_inc(s_wload, 16)
            sp.dma_start(WO[:], wo).then_inc(s_wload, 16)
            sp.dma_start(GW[:], gate_w).then_inc(s_wload, 16)
            sp.dma_start(COND[:], cond).then_inc(s_wload, 16)
            sp.dma_start(CI[:], csti).then_inc(s_wload, 16)
            sp.dma_start(X[:], x.rearrange("b p t -> p b t")).then_inc(s_x0, 16)
            sp.dma_start(MASKB[:].rearrange("p b t -> p (b t)"),
                         cond.rearrange("(a b) t -> a (b t)", a=1).broadcast_to([P, NB * T])).then_inc(s_mask, 16)
            sp.wait_ge(s_pre, 1)
            for k in range(2):
                sp.dma_start(rows_dram[0:TRASH].rearrange("(e k p) c -> k p e c", k=2, p=P)[k],
                             FILL[:, k:k + 1, :].broadcast_to([P, E, ROW])).then_inc(s_rowfill, 16)
            for y in y_dram:
                sp.dma_start(y.rearrange("(n p) t -> p n t", p=P),
                             ZERO[:].unsqueeze(1).broadcast_to([P, YROWS // P, T])).then_inc(s_yzero, 16)
            for i, w in enumerate((sw1, sw3)):
                sp.dma_start(SW13[:, :, i, :], w.rearrange("(k p) n -> p k n", p=P)).then_inc(s_w, 16)
            for i in range(3):
                k = min(P, SI - i * P)
                sp.dma_start(SW2[0:k, i, :], sw2[i * P:i * P + k, :]).then_inc(s_w, 16)
            for e in range(3):
                load_expert(sp, e, e)

        @block.gpsimd
        def _(po):
            order = [0]

            def link(ins):
                order[0] += 1
                ins.then_inc(s_pool, 1)
                po.wait_ge(s_pool, order[0])

            link(nc.gpsimd.memset(ZERO[:], 0.0))
            link(nc.gpsimd.memset(FILL[:], 0.0))
            po.wait_ge(s_wload, 96)
            nc.gpsimd.tensor_copy(FILL[:, :, ROW - 1], CI[:, NB:NB + 2].bitcast(F32)).then_inc(s_pre, 1)
            link(nc.gpsimd.memset(WOP[:], 0.0))
            nc.gpsimd.tensor_copy(WOP[:, :, :, 0:DK], WO[:].rearrange("p (g i d) -> p g i d", g=2, i=4)).then_inc(s_wop, 1)
            po.wait_ge(s_x0, 16)
            po.wait_ge(s_mask, 16)
            nc.gpsimd.tensor_tensor(XM[:, 0:1, :], X[:, 0:1, :], MASKB[:, 0:1, :], ALU.mult).then_inc(s_xm, 1)
            nc.gpsimd.memset(ONES[:], 1.0)
            nc.gpsimd.memset(BEFORE[:], 0.0)
            nc.gpsimd.tensor_tensor(XM[:, 1:NB, :], X[:, 1:NB, :], MASKB[:, 1:NB, :], ALU.mult).then_inc(s_xm, 1)
            po.wait_ge(s_xm, 2)
            po.wait_ge(s_eset, 1)
            po.wait_ge(s_rowfill, 32)

            def batch(b, first, last_done):
                if not first:
                    po.wait_ge(s_pj, 3 * b)
                nc.gpsimd.tensor_copy(XV[:], XM[:, bass.ds(b, 1), :].rearrange("p a t -> p (a t)")).then_inc(s_xv, 1)
                if not first:
                    po.wait_ge(s_pv, 4 * b)
                nc.gpsimd.tensor_copy(
                    VP[:, :, :, DK:32],
                    MASKT[:, :, bass.ds(b, 1)].unsqueeze(3).broadcast_to([P, 2, NH, DK])).then_inc(s_vo, 1)

            def keep_features(b):
                po.wait_ge(s_ytc, b + 1)
                nc.gpsimd.tensor_copy(XFT[:, :, bass.ds(b * P, P)], YT[:]).then_inc(s_xft, 1)

            def scatter(b):
                wait_apart(po, s_slot, b + 1, s_rowfill, 32)
                for k in range(TOPK):
                    po.indirect_dma_start(out=rows_dram, out_offset=bass.IndirectOffsetOnAxis(ap=SLOT[:, k:k + 1], axis=0),
                                          in_=PAY[:], in_offset=None).then_inc(s_scat, 16)

            batch(0, True, False)
            batch(1, False, False)
            keep_features(0)
            with po.Fori(2, NB) as b:
                batch(b, False, False)
                scatter(b - 2)
                keep_features(b - 1)
            scatter(NB - 2)
            keep_features(NB - 1)
            scatter(NB - 1)
            po.wait_ge(s_scat, 16 * TOPK * NB)

        @block.tensor
        def _(pe):
            pe.wait_ge(s_wload, 96)
            nc.tensor.transpose(ps[:, B_PJ, 0:P], WQ[:], IDENT)
            for k in range(2):
                nc.tensor.transpose(ps[:, B_PJ, P + k * E:P + (k + 1) * E], GW[:, k * P:(k + 1) * P], C[0:E, C_ID:C_ID + E])
            for k in range(2):
                nc.tensor.transpose(ps[:, B_PJ, 192 + k * NB:192 + (k + 1) * NB], COND[:, k * P:(k + 1) * P],
                                    C[0:NB, C_ID:C_ID + NB])
            pe.wait_ge(s_wop, 1)
            for g in range(2):
                ins = nc.tensor.transpose(ps[:, B_PJ, 256 + g * P:256 + (g + 1) * P],
                                          WOP[:, g].rearrange("p i d -> p (i d)"), IDENT)
            ins.then_inc(s_tset, 1)

            def project(b, half):
                for i in range(2):
                    ins = nc.tensor.matmul(ps[:, B_PJ, i * T:(i + 1) * T],
                                           WQR[:, 2 * half + i].rearrange("p h r d -> p (h r d)"),
                                           XM[:, bass.ds(b, 1), :].rearrange("p a t -> p (a t)"), start=True, stop=True)
                ins.then_inc(s_pj, 1)

            def project_v(b):
                pe.wait_ge(s_ab, 2 * b + 2)
                pe.wait_ge(s_xv, b + 1)
                for k in range(2):
                    ins = nc.tensor.matmul(ps[:, B_PJ, k * P:(k + 1) * P], XV[:, k * P:(k + 1) * P], WQT[:],
                                           start=True, stop=True)
                ins.then_inc(s_pj, 1)

            def score(b, j, free):
                if free:
                    pe.wait_ge(s_ex, 4 * b + j - 1)
                if j in (0, 2):
                    pe.wait_ge(s_ab, 2 * b + 1 + j // 2)
                for hh in range(2):
                    for k in range(2):
                        ins = nc.tensor.matmul(scores(j % 2)[:, hh, k * T:(k + 1) * T],
                                               QA[64 * hh:64 * hh + 64, j, k * P:(k + 1) * P],
                                               QB[64 * hh:64 * hh + 64, j, :], start=(k == 0), stop=False,
                                               skip_group_check=True)
                ins.then_inc(s_sc, 1)

            def shift(b, j):
                pe.wait_ge(s_nc, 4 * b + j + 1)
                for hh in range(2):
                    ins = nc.tensor.matmul(scores(j % 2)[:, hh, :].rearrange("p (k t) -> p k t", k=2), SEL[:, hh, :],
                                           NMT[:].unsqueeze(1).broadcast_to([4, 2, T]),
                                           start=False, stop=True, skip_group_check=True)
                ins.then_inc(s_sh, 1)

            def weigh(b, j, po_used):
                pe.wait_ge(s_ex, 4 * b + j + 1)
                if j == 0:
                    pe.wait_ge(s_ve, b + 1)
                    pe.wait_ge(s_vo, b + 1)
                    if po_used:
                        pe.wait_ge(s_u, b)
                for hh in range(2):
                    h = 2 * j + hh
                    i, g = h % 4, h // 4
                    for k in range(2):
                        ins = nc.tensor.matmul(ps[32 * i:32 * i + 32, B_PO, g * T:(g + 1) * T], VP[:, k, h, :],
                                               EX[:, j % 2, hh, k, :], start=(k == 0), stop=(k == 1),
                                               skip_group_check=True)
                ins.then_inc(s_pv, 1)

            def turn_max(b, j):
                pe.wait_ge(s_nm, 4 * b + j + 1)
                for k in range(2):
                    ins = nc.tensor.transpose(ps[0:4, B_NM, k * P:(k + 1) * P],
                                              NM2[:, k].rearrange("p r h -> p (r h)"), IDENT)
                ins.then_inc(s_nt, 1)

            def out_project(b, used):
                if used:
                    pe.wait_ge(s_slot, b)
                pe.wait_ge(s_ct, b + 1)
                for g in range(2):
                    ins = nc.tensor.matmul(ps[:, B_FIN, 0:T], WOT[:, g, :], CT[:, g, :], start=(g == 0), stop=(g == 1))
                ins.then_inc(s_wo, 1)

            def turn_y(b):
                pe.wait_ge(s_y, b + 1)
                for k in range(2):
                    ins = nc.tensor.transpose(ps[:, B_FIN, T + k * P:T + (k + 1) * P], PAY[:, k * P:(k + 1) * P], IDENT)
                ins.then_inc(s_yt, 1)

            def logits(b):
                pe.wait_ge(s_ytc, b + 1)
                for k in range(2):
                    ins = nc.tensor.matmul(ps[:, B_FIN, 0:E], YT[:, k, :], GWT[:, k, :], start=(k == 0), stop=(k == 1))
                ins.then_inc(s_lg, 1)

            def count(b):
                pe.wait_ge(s_ch, b + 1)
                nc.tensor.matmul(ps[:, B_FIN, E:2 * E], C[:, C_UP:C_UP + P], CHOSEN[:], start=True, stop=False)
                nc.tensor.matmul(ps[:, B_FIN, E:2 * E], ONES[:], BEFORE[:], start=False, stop=True).then_inc(s_ct2, 1)

            def step(b, j, has_prev, has_prev2, has_next, first=False):
                shift(b, j)
                if j < 3:
                    score(b, j + 1, not (first and j == 0))
                elif has_next:
                    score(b + 1, 0, True)
                if j > 0:
                    weigh(b, j - 1, has_prev)
                elif has_prev:
                    weigh(b - 1, 3, True)
                if j < 3:
                    turn_max(b, j + 1)
                elif has_next:
                    turn_max(b + 1, 0)
                if j == 0:
                    project_v(b)
                    if has_prev2:
                        count(b - 2)
                if j == 1:
                    if has_next:
                        pe.wait_ge(s_ve, b + 1)
                        project(b + 1, 0)
                    if has_prev:
                        out_project(b - 1, has_prev2)
                if j == 2 and has_prev:
                    turn_y(b - 1)
                if j == 3:
                    if has_next:
                        pe.wait_ge(s_ab, 2 * b + 3)
                        project(b + 1, 1)
                    if has_prev:
                        logits(b - 1)

            pe.wait_ge(s_wqr, 3)
            pe.wait_ge(s_xm, 1)
            project(0, 0)
            pe.wait_ge(s_ab, 1)
            project(0, 1)
            pe.wait_ge(s_xm, 2)
            pe.wait_ge(s_eset, 2)
            score(0, 0, False)
            turn_max(0, 0)
            pe.wait_ge(s_xs, 1)
            for g in range(2):
                nc.tensor.matmul(ps[:, B_FIN, g * NB:(g + 1) * NB], WQG[:, g].rearrange("p i d -> p (i d)"), XS[:, 0, :],
                                 start=True, stop=False)
                ins = nc.tensor.matmul(ps[:, B_FIN, g * NB:(g + 1) * NB], C[:, C_DEN:C_DEN + P], XS[:, 1, :],
                                       start=False, stop=True)
            ins.then_inc(s_svp, 1)
            pe.wait_ge(s_sv, 1)
            for j in range(4):
                step(0, j, False, False, True, first=True)
            for j in range(4):
                step(1, j, True, False, True)
            with pe.Fori(2, NB - 1) as b:
                for j in range(4):
                    step(b, j, True, True, True)
            for j in range(4):
                step(NB - 1, j, True, True, False)
            weigh(NB - 1, 3, True)
            count(NB - 2)
            out_project(NB - 1, True)
            turn_y(NB - 1)
            logits(NB - 1)
            count(NB - 1)

        @block.scalar
        def _(act):
            act.wait_ge(s_tset, 1)
            nc.scalar.activation(WQT[:], ps[:, B_PJ, 0:P], ACT.Copy).then_inc(s_wqr, 1)
            nc.scalar.activation(MASKT[:].rearrange("p k b -> p (k b)"), ps[:, B_PJ, 192:192 + 2 * NB], ACT.Copy).then_inc(s_eset, 1)
            nc.scalar.activation(GWT[:].rearrange("p k b -> p (k b)"), ps[:, B_PJ, P:P + 2 * E], ACT.Copy)
            nc.scalar.activation(WOT[:].rearrange("p g n -> p (g n)"), ps[:, B_PJ, 256:512], ACT.Copy).then_inc(s_wqr, 1)
            nc.scalar.activation(SEL[:].rearrange("p h n -> p (h n)"), C[0:4, C_SEL:C_SEL + 2 * P], ACT.Copy).then_inc(s_eset, 1)

            def high(b, half, first=False):
                act.wait_ge(s_pj, 3 * b + 1 + half)
                if not first:
                    act.wait_ge(s_ab, 2 * b + half)
                nc.scalar.activation(HI[:].rearrange("p i t -> p (i t)"), ps[:, B_PJ, :], ACT.Copy).then_inc(s_hi, 1)

            def negmax(b, j):
                act.wait_ge(s_nt, 4 * b + j + 1)
                nc.scalar.activation(NMT[:], ps[0:4, B_NM, 0:T], ACT.Copy).then_inc(s_nc, 1)

            def exps(b, j, used):
                act.wait_ge(s_sh, 4 * b + j + 1)
                if used:
                    act.wait_ge(s_pv, 4 * b + j - 1)
                nc.scalar.activation(EX[:, j % 2].rearrange("p h k t -> p h (k t)"), scores(j % 2), ACT.Exp,
                                     scale=float(DK) ** -0.5).then_inc(s_ex, 1)

            def values(b, used):
                act.wait_ge(s_pj, 3 * b + 3)
                if used:
                    act.wait_ge(s_pv, 4 * b)
                nc.scalar.activation(VP[:, :, :, 0:DK],
                                     ps[:, B_PJ, 0:2 * P].rearrange("p (k h d) -> p k h d", k=2, h=NH),
                                     ACT.Copy).then_inc(s_ve, 1)

            def keep_y(b, used):
                act.wait_ge(s_wo, b + 1)
                if used:
                    act.wait_ge(s_scat, 16 * TOPK * b)
                nc.scalar.activation(PAY[:, 0:T], ps[:, B_FIN, 0:T], ACT.Copy).then_inc(s_y, 1)

            def keep_yt(b, used):
                act.wait_ge(s_yt, b + 1)
                if used:
                    act.wait_ge(s_xft, b)
                nc.scalar.activation(YT[:].rearrange("p k n -> p (k n)"), ps[:, B_FIN, T:2 * T], ACT.Copy).then_inc(s_ytc, 1)

            def router_exp(b):
                act.wait_ge(s_top, b + 1)
                nc.scalar.activation(ES[:], LG[:], ACT.Exp, bias=NTOP[:], accum_out=ESUM[:]).then_inc(s_es, 1)

            def step(b, j, has_prev, has_prev2, has_next, first=False):
                exps(b, j, has_prev or j >= 2)
                if j < 3:
                    negmax(b, j + 1)
                elif has_next:
                    negmax(b + 1, 0)
                if j == 0:
                    values(b, has_prev)
                    if has_prev2:
                        router_exp(b - 2)
                if j == 1:
                    if has_next:
                        high(b + 1, 0)
                    if has_prev:
                        keep_y(b - 1, has_prev2)
                if j == 2 and has_prev:
                    keep_yt(b - 1, has_prev2)
                if j == 3 and has_next:
                    high(b + 1, 1)

            high(0, 0, True)
            high(0, 1)
            negmax(0, 0)
            act.wait_ge(s_svp, 1)
            nc.scalar.activation(SV[:].rearrange("p g b -> p (g b)"), ps[:, B_FIN, 0:2 * NB], ACT.Copy).then_inc(s_sv, 1)
            for j in range(4):
                step(0, j, False, False, True, first=True)
            for j in range(4):
                step(1, j, True, False, True)
            with act.Fori(2, NB - 1) as b:
                for j in range(4):
                    step(b, j, True, True, True)
            for j in range(4):
                step(NB - 1, j, True, True, False)
            router_exp(NB - 2)
            keep_y(NB - 1, True)
            keep_yt(NB - 1, True)
            router_exp(NB - 1)

        @block.vector
        def _(dve):
            state = {"base": 0, "k": 0}

            def link(ins, apart=False):
                state["k"] += 1
                ins.then_inc(s_dve, 1)
                if apart:
                    wait_apart(dve, s_dve, state["base"] + state["k"], s_mask, 16)
                else:
                    dve.wait_ge(s_dve, state["base"] + state["k"])

            dve.wait_ge(s_wqr, 1)
            nc.vector.tensor_copy(WQR[:].rearrange("p j h r d -> p (j h) r d"),
                                  WQT[:].rearrange("p (h d) -> p h d", h=NH).unsqueeze(2).broadcast_to([P, NH, 4, DK])
                                  ).then_inc(s_wqr, 1)

            def operands(b, half, used):
                dve.wait_ge(s_hi, 2 * b + 1 + half)
                if used:
                    dve.wait_ge(s_sc, 4 * b - 2 + 2 * half)
                q = ps[:, B_PJ, :].rearrange("p (i t) -> p i t", i=2)
                for n, dst in enumerate((QA, QB)):
                    ins = nc.vector.scalar_tensor_tensor(
                        out=dst[:, 2 * half:2 * half + 2, :], in0=HI[:].bitcast(F32),
                        scalar=C[:, C_SPLIT + n:C_SPLIT + n + 1], in1=q, op0=ALU.mult, op1=ALU.add)
                ins.then_inc(s_ab, 1)

            def negmax(b, j, used):
                dve.wait_ge(s_sc, 4 * b + j + 1)
                link(nc.vector.tensor_reduce(NEGMAX[:], scores(j % 2).rearrange("p h (k t) -> p h k t", k=2),
                                             AX.X, ALU.max, negate=True))
                nm = NEGMAX[:].rearrange("p h k -> p k h")
                if used:
                    dve.wait_ge(s_nt, 4 * b + j)
                link(nc.vector.tensor_copy(NM2[:, :, 0, :].bitcast(F32R), nm))
                nc.vector.tensor_tensor(NM2[:, :, 1, :], nm, NM2[:, :, 0, :], ALU.subtract).then_inc(s_nm, 1)

            def context(b):
                dve.wait_ge(s_pv, 4 * b + 4)
                for g in range(2):
                    ins = nc.vector.scalar_tensor_tensor(
                        out=U[:, g, :], in0=INV[:, bass.ds(b, 1), :].rearrange("p a t -> p (a t)"),
                        scalar=SV[:, g, bass.ds(b, 1)], in1=ps[:, B_PO, g * T:(g + 1) * T], op0=ALU.mult, op1=ALU.add)
                ins.then_inc(s_u, 1)
                wait_apart(dve, s_u, b + 1, s_mask, 16)
                link(nc.vector.stream_shuffle(DEN[:].rearrange("p g t -> p (g t)"), U[:].rearrange("p g t -> p (g t)"),
                                              [DK + i % DK for i in range(32)]))
                link(nc.vector.reciprocal(DEN[:], DEN[:]))
                nc.vector.tensor_tensor(CT[:], U[:], DEN[:], ALU.mult).then_inc(s_ct, 1)

            def choose(b):
                dve.wait_ge(s_lg, b + 1)
                link(nc.vector.tensor_copy(LG[:], ps[:, B_FIN, 0:E]), apart=True)
                link(nc.vector.max(TOP[:], LG[:]))
                nc.vector.tensor_scalar(NTOP[:], TOP[:, 0:1], -1.0, None, ALU.mult).then_inc(s_top, 1)
                link(nc.vector.max_index(TOPI[:], TOP[:], LG[:]))
                link(nc.vector.tensor_copy(TOPF[:], TOPI[:]))
                link(nc.vector.tensor_tensor(ONEH[:], C[:, C_IOTA:C_IOTA + E].unsqueeze(1).broadcast_to([P, TOPK, E]),
                                             TOPF[:, 0:TOPK].unsqueeze(2).broadcast_to([P, TOPK, E]), ALU.is_equal))
                nc.vector.tensor_reduce(CHOSEN[:], ONEH[:].rearrange("p k e -> p e k"), AX.X, ALU.add).then_inc(s_ch, 1)

            def place(b, used):
                dve.wait_ge(s_ct2, b + 1)
                link(nc.vector.tensor_tensor(PICK[:], ONEH[:], ps[:, B_FIN, E:2 * E].unsqueeze(1).broadcast_to([P, TOPK, E]),
                                             ALU.mult))
                link(nc.vector.tensor_reduce(PLACE[:], PICK[:], AX.X, ALU.add))
                nc.vector.tensor_scalar(FITS[:], PLACE[:], float(CAP), None, ALU.is_lt)
                link(nc.vector.scalar_tensor_tensor(out=SLOTF[:], in0=TOPF[:, 0:TOPK], scalar=float(CAP), in1=PLACE[:],
                                                    op0=ALU.mult, op1=ALU.add))
                link(nc.vector.scalar_tensor_tensor(out=SLOTF[:], in0=SLOTF[:], scalar=C[:, C_TRASH:C_TRASH + 1],
                                                    in1=FITS[:], op0=ALU.subtract, op1=ALU.mult))
                if used:
                    dve.wait_ge(s_scat, 16 * TOPK * b)
                nc.vector.tensor_scalar(SLOT[:], SLOTF[:], C[:, C_TRASH:C_TRASH + 1], None, ALU.add)
                nc.vector.tensor_tensor(BEFORE[:], BEFORE[:], CHOSEN[:], ALU.add)
                nc.vector.tensor_copy(PAY[:, ROW - 1:ROW], CI[:, bass.ds(b, 1)].bitcast(F32))
                dve.wait_ge(s_es, b + 1)
                link(nc.vector.reciprocal(RSUM[:], ESUM[:]))
                nc.vector.tensor_scalar(PAY[:, T:T + E], ES[:], RSUM[:, 0:1], None, ALU.mult).then_inc(s_slot, 1)

            def step(b, j, has_prev, has_prev2, has_next, first=False):
                if j == 0:
                    if has_prev:
                        operands(b, 1, True)
                    if has_prev2:
                        choose(b - 2)
                if j == 2 and has_next:
                    operands(b + 1, 0, True)
                if j < 3:
                    negmax(b, j + 1, True)
                elif has_next:
                    negmax(b + 1, 0, True)
                if j == 0 and has_prev:
                    context(b - 1)
                if j == 0 and has_prev2:
                    place(b - 2, True)

            operands(0, 0, False)
            operands(0, 1, False)
            dve.wait_ge(s_mask, 16)
            dve.wait_ge(s_x0, 16)
            negmax(0, 0, False)
            link(nc.vector.tensor_scalar(INV[:], MASKB[:], -1.0, 1.0, ALU.mult, ALU.add))
            link(nc.vector.tensor_tensor(XI[:], X[:], INV[:], ALU.mult))
            nc.vector.tensor_reduce(XS[:, 0, :], XI[:], AX.X, ALU.add)
            nc.vector.tensor_reduce(XS[:, 1, :], INV[:], AX.X, ALU.add)
            link(nc.vector.memset(WQG[:], 0.0))
            nc.vector.tensor_copy(WQG[:, :, :, 0:DK], WQT[:].rearrange("p (g i d) -> p g i d", g=2, i=4)).then_inc(s_xs, 1)
            dve.wait_ge(s_sv, 1)
            dve.wait_ge(s_pool, 3)
            for j in range(4):
                step(0, j, False, False, True, first=True)
            for j in range(4):
                step(1, j, True, False, True)
            base, per = state["k"], PER_BATCH
            with dve.Fori(2, NB - 1) as b:
                state["base"], state["k"] = base + (b - 2) * per, 0
                for j in range(4):
                    step(b, j, True, True, True)
                assert state["k"] == per, state["k"]
            state["base"], state["k"] = base + (NB - 3) * per, 0
            for j in range(4):
                step(NB - 1, j, True, True, False)
            choose(NB - 2)
            context(NB - 1)
            place(NB - 2, True)
            choose(NB - 1)
            place(NB - 1, True)


PER_BATCH = 20


def experts(nc, sb, sem, ps, rows_dram, y_dram, X, XFT, SW13, SW2, W1, W3, W2A, W2B, C, CI, IDENT,
            s_w, s_ew, s_yzero, load_expert, out):
    TAIL = INTER - HEADW
    NG = 3
    GW_ = [min(P, SI - i * P) for i in range(NG)]
    CH = TOK // T
    with ExitStack() as ctx:
        def sb(name, shape, dt=F32):
            return ctx.enter_context(nc.sbuf_tensor(name, shape, dt))

        RING = len(W1)
        XB = [sb(f"XB{i}", [P, 2, ROW]) for i in range(RING)]
        META = [sb(f"META{i}", [P, 2, 2]) for i in range(RING)]
        XT = [sb(f"XT{i}", [P, 2, CAP]) for i in range(2)]
        SG = [sb(f"SG{i}", [P, 2, CAP]) for i in range(2)]
        HA = [sb(f"HA{i}", [P, CAP]) for i in range(2)]
        HB = [sb(f"HB{i}", [TAIL, CAP]) for i in range(2)]
        O = [sb(f"O{i}", [P, 2, T]) for i in range(RING)]
        SGS = [sb(f"SGS{i}", [P, T]) for i in range(2)]
        HS = sb("HS", [P, NG, T])
        YS = sb("YS", [P, 2, NB, T])

        s_sup = sem("shared_up_ready")
        s_ssg = sem("shared_silu_ready")
        s_sh = sem("shared_h_ready")
        s_sdn = sem("shared_down_ready")
        s_res = sem("residual_ready")
        s_xb = [sem(f"expert_rows_loaded{i}") for i in range(RING)]
        s_tr = sem("rows_transposed")
        s_xt = sem("xt_ready")
        s_meta = sem("meta_ready")
        s_up = sem("up_ready")
        s_sg = sem("silu_ready")
        s_h = sem("h_ready")
        s_dn = sem("down_ready")
        s_o = sem("weighted_ready")
        s_acc = [sem(f"results_added{i}") for i in range(2)]
        s_yl = sem("y_loaded")
        s_fin = sem("final_ready")
        s_final_chain = sem("y_halves_added")
        s_out = sem("stored")

        B_UP, B_T, B_DN = 0, 4, 6

        block = ctx.enter_context(nc.Block())

        @block.sync
        def _(sp):
            def load_rows(e, m):
                sp.dma_start(XB[m][:], rows_dram[bass.ds(e * CAP, CAP)].rearrange("(k p) c -> p k c", p=P)).then_inc(s_xb[m], 16)

            for e in range(3):
                load_rows(e, e)
            load_rows(3, 3)
            load_expert(sp, 3, 3)
            with sp.Fori(0, (E - 4) // 4) as i:
                for m in range(4):
                    sp.wait_ge(s_meta, 4 * i + m + 1)
                    sp.wait_ge(s_tr, 4 * i + m + 1)
                    load_rows(4 * i + m + 4, m)
                    sp.wait_ge(s_dn, 4 * i + m + 1)
                    load_expert(sp, 4 * i + m + 4, m)
            for par in range(2):
                sp.wait_ge(s_acc[par], 16 * E)
            for n in range(2):
                sp.dma_start(YS[:, n], y_dram[n][0:TOK].rearrange("(b p) t -> p b t", p=P)).then_inc(s_yl, 16)
            for n in range(2):
                sp.wait_ge(s_fin, n + 1)
                h = NB // 2
                sp.dma_start(out[n * h:(n + 1) * h].rearrange("b p t -> p b t"), X[:, n * h:(n + 1) * h, :]).then_inc(s_out, 16)
            sp.wait_ge(s_out, 32)

        @block.gpsimd
        def _(po):
            po.wait_ge(s_yzero, 32)
            def add(e, m, par, used):
                if used:
                    wait_apart(po, s_acc[par], 16 * (e - m) + 32 * (m // 2), s_yzero, 32)
                wait_apart(po, s_o, e + 1, s_yzero, 32)
                for k in range(2):
                    po.indirect_dma_start(out=y_dram[par], out_offset=bass.IndirectOffsetOnAxis(
                        ap=META[m][:, k, 1:2].bitcast(I32), axis=0), in_=O[m][:, k, :], in_offset=None,
                        compute_op=ALU.add).then_inc(s_acc[par], 16)

            for e in range(4):
                add(e, e, e % 2, e >= 2)
            with po.Fori(1, E // 4) as i:
                for m in range(4):
                    add(4 * i + m, m, m % 2, True)
            for par in range(2):
                po.wait_ge(s_acc[par], 16 * E)

        @block.tensor
        def _(pe):
            pe.wait_ge(s_w, 80)
            with pe.Fori(0, CH) as c:
                for i in range(NG):
                    n = i % 2
                    if i == 2:
                        pe.wait_ge(s_sh, NG * c + 1)
                    for u in range(2):
                        for k in range(2):
                            ins = nc.tensor.matmul(ps[0:GW_[i], B_UP + 2 * n + u, 0:T], SW13[:, k, u, i * P:i * P + GW_[i]],
                                                   XFT[:, k, bass.ds(c * T, T)], start=(k == 0), stop=(k == 1))
                    ins.then_inc(s_sup, 1)
                pe.wait_ge(s_sh, NG * c + NG)
                for st in range(2):
                    for i in range(NG):
                        ins = nc.tensor.matmul(ps[:, B_DN + st, 0:T], HS[0:GW_[i], i, st * P:(st + 1) * P], SW2[0:GW_[i], i, :],
                                               start=(i == 0), stop=(i == NG - 1))
                ins.then_inc(s_sdn, 1)
                pe.wait_ge(s_res, c + 1)

            def turn(e, m, free):
                pe.wait_ge(s_xb[m], 16 * (e // 4) + 16 if isinstance(e, int) else (e - m) * 4 + 16)
                if free:
                    pe.wait_ge(s_xt, e - 1)
                for st in range(2):
                    for k in range(2):
                        ins = nc.tensor.transpose(ps[:, B_T + m % 2, k * CAP + st * P:k * CAP + (st + 1) * P],
                                                  XB[m][:, st, k * P:(k + 1) * P], IDENT)
                ins.then_inc(s_tr, 1)

            def up(e, m, free):
                pe.wait_ge(s_ew[m], 80 * (e // 4) + 80 if isinstance(e, int) else (e - m) * 20 + 80)
                pe.wait_ge(s_xt, e + 1)
                if free:
                    pe.wait_ge(s_h, e - 1)
                b0 = B_UP + 2 * (m % 2)
                for lhs, dst in ((lambda k: W1[m][:, k, 0:P], ps[:, b0, 0:CAP]),
                                 (lambda k: W1[m][:, k, HEADW:INTER + TAIL], ps[:, b0, CAP:2 * CAP]),
                                 (lambda k: W3[m][:, k, 0:P], ps[:, b0 + 1, 0:CAP])):
                    for k in range(2):
                        ins = nc.tensor.matmul(dst, lhs(k), XT[m % 2][:, k, :], start=(k == 0), stop=(k == 1))
                ins.then_inc(s_up, 1)

            def down(e, m, free):
                pe.wait_ge(s_h, e + 1)
                if free:
                    pe.wait_ge(s_o, e - 1)
                for st in range(2):
                    cols = slice(st * P, (st + 1) * P)
                    dst = ps[:, B_DN + m % 2, st * T:(st + 1) * T]
                    nc.tensor.matmul(dst, HA[m % 2][0:HEADW, cols], W2A[m][:], start=True, stop=False)
                    ins = nc.tensor.matmul(dst, HB[m % 2][:, cols], W2B[m][:], start=False, stop=True)
                ins.then_inc(s_dn, 1)

            turn(0, 0, False)
            turn(1, 1, False)
            up(0, 0, False)
            turn(2, 2, True)
            up(1, 1, False)
            down(0, 0, False)
            turn(3, 3, True)
            up(2, 2, True)
            down(1, 1, False)
            with pe.Fori(0, (E - 4) // 4) as i:
                for m in range(4):
                    turn(4 * i + m + 4, m, True)
                    up(4 * i + m + 3, (m + 3) % 4, True)
                    down(4 * i + m + 2, (m + 2) % 4, True)
            up(E - 1, 3, True)
            down(E - 2, 2, True)
            down(E - 1, 3, True)

        @block.scalar
        def _(act):
            with act.Fori(0, CH) as c:
                for i in range(NG):
                    act.wait_ge(s_sup, NG * c + i + 1)
                    if i == 2:
                        act.wait_ge(s_sh, NG * c + 1)
                    nc.scalar.activation(SGS[i % 2][0:GW_[i], :], ps[0:GW_[i], B_UP + 2 * (i % 2), 0:T], ACT.Silu).then_inc(s_ssg, 1)

            def rows(e, m, used):
                act.wait_ge(s_tr, e + 1)
                if used:
                    act.wait_ge(s_up, e - 1)
                nc.scalar.activation(XT[m % 2][:].rearrange("p k n -> p (k n)"), ps[:, B_T + m % 2, :], ACT.Copy).then_inc(s_xt, 1)

            def silu(e, m, used):
                act.wait_ge(s_up, e + 1)
                if used:
                    act.wait_ge(s_h, e - 1)
                nc.scalar.activation(SG[m % 2][:].rearrange("p k n -> p (k n)"), ps[:, B_UP + 2 * (m % 2), :], ACT.Silu).then_inc(s_sg, 1)

            rows(0, 0, False)
            rows(1, 1, False)
            silu(0, 0, False)
            rows(2, 2, True)
            silu(1, 1, False)
            rows(3, 3, True)
            silu(2, 2, True)
            with act.Fori(0, (E - 4) // 4) as i:
                for m in range(4):
                    rows(4 * i + m + 4, m, True)
                    silu(4 * i + m + 3, (m + 3) % 4, True)
            silu(E - 1, 3, True)

        @block.vector
        def _(dve):
            with dve.Fori(0, CH) as c:
                for i in range(NG):
                    dve.wait_ge(s_ssg, NG * c + i + 1)
                    nc.vector.tensor_tensor(HS[0:GW_[i], i, :], SGS[i % 2][0:GW_[i], :], ps[0:GW_[i], B_UP + 2 * (i % 2) + 1, 0:T],
                                            ALU.mult).then_inc(s_sh, 1)
                dve.wait_ge(s_sdn, c + 1)
                xc = X[:, bass.ds(c * 2, 2), :]
                nc.vector.tensor_tensor(xc, xc, ps[:, B_DN:B_DN + 2, 0:T], ALU.add).then_inc(s_res, 1)

            def meta(e, m, used):
                dve.wait_ge(s_xb[m], 16 * (e // 4) + 16 if isinstance(e, int) else (e - m) * 4 + 16)
                if used:
                    dve.wait_ge(s_acc[m % 2], 16 * (e - m) - 32 + 32 * (m // 2))
                nc.vector.tensor_copy(META[m][:, :, 1:2], XB[m][:, :, ROW - 1:ROW])
                nc.vector.tensor_copy(META[m][:, :, 0:1], XB[m][:, :, bass.ds(e + T, 1)]).then_inc(s_meta, 1)

            def hidden(e, m):
                dve.wait_ge(s_sg, e + 1)
                b0 = B_UP + 2 * (m % 2)
                nc.vector.tensor_tensor(HA[m % 2][:], SG[m % 2][:, 0, :], ps[:, b0 + 1, 0:CAP], ALU.mult)
                nc.vector.tensor_tensor(HB[m % 2][:], SG[m % 2][0:TAIL, 1, :], ps[64:64 + TAIL, b0, CAP:2 * CAP],
                                        ALU.mult).then_inc(s_h, 1)

            def weighted(e, m):
                dve.wait_ge(s_dn, e + 1)
                dve.wait_ge(s_meta, e + 1)
                for st in range(2):
                    ins = nc.vector.tensor_scalar(O[m][:, st, :], ps[:, B_DN + m % 2, st * T:(st + 1) * T],
                                                  META[m][:, st, 0:1], None, ALU.mult)
                ins.then_inc(s_o, 1)

            meta(0, 0, False)
            meta(1, 1, False)
            hidden(0, 0)
            meta(2, 2, False)
            hidden(1, 1)
            weighted(0, 0)
            meta(3, 3, False)
            hidden(2, 2)
            weighted(1, 1)
            with dve.Fori(0, (E - 4) // 4) as i:
                for m in range(4):
                    hidden(4 * i + m + 3, (m + 3) % 4)
                    weighted(4 * i + m + 2, (m + 2) % 4)
                    meta(4 * i + m + 4, m, True)
            hidden(E - 1, 3)
            weighted(E - 2, 2)
            weighted(E - 1, 3)
            dve.wait_ge(s_yl, 32)
            h = NB // 2
            dve.wait_ge(s_res, CH)
            for n in range(2):
                half = slice(n * h, (n + 1) * h)
                nc.vector.tensor_tensor(YS[:, 0, half, :], YS[:, 0, half, :], YS[:, 1, half, :], ALU.add).then_inc(s_final_chain, 1)
                dve.wait_ge(s_final_chain, n + 1)
                nc.vector.tensor_tensor(X[:, half, :], X[:, half, :], YS[:, 0, half, :], ALU.add).then_inc(s_fin, 1)


_INS = ["x", "cond_2048", "L0_cond_Wq", "L0_cond_Wo", "L0_ffn_gate_w", "L0_ffn_w1", "L0_ffn_w2", "L0_ffn_w3",
        "L0_ffn_sw1", "L0_ffn_sw2", "L0_ffn_sw3"]


def constants():
    import numpy as np

    p = np.arange(P)
    c = np.zeros((P, NCONST), np.float32)
    c[:, C_ID:C_ID + P] = np.eye(P)
    c[:, C_UP:C_UP + P] = p[:, None] < p[None, :]
    c[0, C_DEN:C_DEN + P] = p % 32 >= DK
    for part in range(2):
        for h in range(2):
            c[2 * part + h, C_SEL + h * P:C_SEL + (h + 1) * P] = 1
    c[:, C_IOTA:C_IOTA + E] = np.arange(E)
    c[:, C_SPLIT] = -(p // 32 % 2)
    c[:, C_SPLIT + 1] = -(p // 16 % 2)
    c[:, C_TRASH] = TRASH + p
    i = np.zeros((P, NB + 2), np.int32)
    i[:, :NB] = p[:, None] + P * np.arange(NB)
    i[:, NB:] = TOK + p[:, None] + P * np.arange(2)
    return c, i


def kernel(**inputs):
    import numpy as _np
    import concourse.bacc as _bacc
    from concourse import mybir as _mybir
    from concourse.bass_utils import run_bass_kernel_spmd as _run

    nc = _bacc.Bacc("TRN2", target_bir_lowering=False, num_devices=1)
    arrays, args = {}, []
    given = [_np.ascontiguousarray(inputs[name]) for name in _INS] + list(constants())
    for name, a in zip(_INS + ["constants", "token_numbers"], given):
        arrays[f"in_{name}"] = a
        args.append(nc.dram_tensor(f"in_{name}", a.shape, _mybir.dt.from_np(a.dtype), kind="ExternalInput").ap())
    out = nc.dram_tensor("out_0", (NB, D, T), _mybir.dt.float32, kind="ExternalOutput").ap()
    build(nc, *args, out)
    r = _run(nc, [arrays], core_ids=[0])
    return r.results[0]["out_0"]
```

```python
from contextlib import ExitStack

import concourse.bass as bass
from concourse import mybir

F32 = mybir.dt.float32
F32R = mybir.dt.float32r
I32 = mybir.dt.int32
U32 = mybir.dt.uint32
ALU = mybir.AluOpType
ACT = mybir.ActivationFunctionType
AX = mybir.AxisListType

P = 128
NB, D, T = 8, 128, 256
NH, DK = 8, 16
E, TOPK, CAP = 32, 6, 256
INTER, SI = 176, 352
TOK = NB * D
STEPS = NB * NH // 2
ROW = T + E + 1
TRASH = E * CAP
YROWS = TOK + CAP
DV = DK + 1
HL = 32 + NB
HEADW = 112

C_ID, C_UP = 0, 128
C_SEL = 256
C_IOTA = C_SEL + 4 * P
C_SPLIT = C_IOTA + E
C_TRASH = C_SPLIT + 2
C_DIAG = C_TRASH + 1
NCONST = C_DIAG + NB


def wait_apart(engine, signal, value, met, met_value):
    if not isinstance(value, int):
        register = engine.alloc_register()
        engine.reg_add(register, value, 0)
        value = register
    engine.wait_ge(met, met_value)
    engine.wait_ge(signal, value)


def build(nc, x, cond, wq, wo, gate_w, w1, w2, w3, sw1, sw2, sw3, cst, csti, out):
    ctx = ExitStack()
    with ctx:
        def sb(name, shape, dt=F32):
            return ctx.enter_context(nc.sbuf_tensor(name, shape, dt))

        def sem(name):
            return ctx.enter_context(nc.semaphore(name))

        rows_dram = nc.dram_tensor("expert_rows", [TRASH + P, ROW], F32).ap()
        y_dram = [nc.dram_tensor(f"y{i}", [YROWS, T], F32).ap() for i in range(2)]

        ps = ctx.enter_context(nc.psum_tensor("ps", [P, 8, 512], F32))

        X = sb("X", [P, NB, T])
        XFT = sb("XFT", [P, 2, TOK])
        SW13 = sb("SW13", [P, 2, 2, SI])
        SW2 = sb("SW2", [P, 3, T])
        RING = 4
        TAIL = INTER - HEADW
        W1 = [sb(f"W1_{i}", [P, 2, INTER + TAIL]) for i in range(RING)]
        W3 = [sb(f"W3_{i}", [P, 2, INTER]) for i in range(RING)]
        W2A = [sb(f"W2A_{i}", [HEADW, T]) for i in range(RING)]
        W2B = [sb(f"W2B_{i}", [INTER - HEADW, T]) for i in range(RING)]
        XB = [sb(f"XB{i}", [P, 2, ROW]) for i in range(RING)]
        C = sb("C", [P, NCONST])
        CI = sb("CI", [P, NB + 2], I32)
        IDENT = C[:, C_ID:C_ID + P]
        ZERO = sb("ZERO", [P, T])
        FILL = sb("FILL", [P, 2, ROW])

        s_w = sem("shared_weights_loaded")
        s_ew = [sem(f"expert_weights_loaded{i}") for i in range(RING)]
        s_xb = [sem(f"expert_rows_loaded{i}") for i in range(RING)]
        s_yzero = sem("y_zeroed")

        def load_expert(sp, e, m):
            w3e = w3[e].rearrange("(k p) n -> p k n", p=P)
            sp.dma_start(W1[m][:, :, 0:INTER], w1[e].rearrange("(k p) n -> p k n", p=P)).then_inc(s_ew[m], 16)
            sp.dma_start(W1[m][:, :, INTER:INTER + TAIL], w3e[:, :, HEADW:INTER]).then_inc(s_ew[m], 16)
            sp.dma_start(W3[m][:], w3e).then_inc(s_ew[m], 16)
            sp.dma_start(W2A[m][:], w2[e, 0:HEADW, :]).then_inc(s_ew[m], 16)
            sp.dma_start(W2B[m][:], w2[e, HEADW:INTER, :]).then_inc(s_ew[m], 16)

        def load_rows(sp, e, m):
            sp.dma_start(XB[m][:], rows_dram[bass.ds(e * CAP, CAP)].rearrange("(k p) c -> p k c", p=P)).then_inc(s_xb[m], 16)

        attention(nc, sb, sem, ps, x, cond, wq, wo, gate_w, sw1, sw2, sw3, cst, csti,
                  rows_dram, y_dram, X, XFT, SW13, SW2, C, CI, IDENT, ZERO, FILL, s_w, s_yzero,
                  load_expert, load_rows)
        experts(nc, sb, sem, ps, y_dram, X, XB, W1, W3, W2A, W2B, IDENT, s_ew, s_xb, s_yzero,
                load_expert, load_rows, out)


def attention(nc, sb, sem, ps, x, cond, wq, wo, gate_w, sw1, sw2, sw3, cst, csti,
              rows_dram, y_dram, X, XFT, SW13, SW2, C, CI, IDENT, ZERO, FILL, s_w, s_yzero,
              load_expert, load_rows):
    with ExitStack() as ctx:
        def sb(name, shape, dt=F32):
            return ctx.enter_context(nc.sbuf_tensor(name, shape, dt))

        MASKB = sb("MASKB", [P, NB, T])
        XM = sb("XM", [P, NB, T])
        XI = sb("XI", [P, NB, T])
        INVC = sb("INVC", [HL, T])
        INVD = sb("INVD", [HL, NB, T], F32R)
        XV = sb("XV", [P, T])
        COND = sb("COND", [HL, T])
        WQ = sb("WQ", [P, D])
        WO = sb("WO", [P, D])
        WOT = sb("WOT", [P, P])
        GW = sb("GW", [E, T])
        GWT = sb("GWT", [P, 2, E])
        MASKT = sb("MASKT", [P, 2, NB])
        WQT = sb("WQT", [P, D])
        WQR = sb("WQR", [P, 4, 2, 4, DK])
        SEL = sb("SEL", [8, 2, 2, P], F32R)
        UP = sb("UP", [P, P], F32R)
        MASKED = sb("MASKED", [NB, 1])
        XS = sb("XS", [P, HL])
        SV = sb("SV", [HL, 2, 4, 32], F32R)
        HI = sb("HI", [P, 2, T], F32R)
        QA = sb("QA", [P, 4, T], F32R)
        QB = sb("QB", [P, 4, T], F32R)
        VS = sb("VS", [P, 2, NH, DV])
        VP = sb("VP", [P, 2, NH, DV])
        EX = sb("EX", [P, 4, 2, 2, T])
        NEGMAX = sb("NEGMAX", [P, 2, 2])
        NM2 = sb("NM2", [P, 2, 2, 2])
        NMT = sb("NMT", [8, P], F32R)
        U = sb("U", [P, 2, T])
        RDEN = sb("RDEN", [P, 2 * NH, 1])
        CTX = sb("CTX", [P, 2, P])
        CTT = sb("CTT", [P, T])
        PAY = sb("PAY", [P, ROW])
        YT = sb("YT", [P, 2, P])
        LG = sb("LG", [P, E])
        TOP = sb("TOP", [P, 8])
        TOPI = sb("TOPI", [P, 8], U32)
        TOPF = sb("TOPF", [P, 8])
        NTOP = sb("NTOP", [P, 1])
        ESUM = sb("ESUM", [P, 1])
        RSUM = sb("RSUM", [P, 1])
        ES = sb("ES", [P, E])
        ONEH = sb("ONEH", [P, TOPK, E])
        PICK = sb("PICK", [P, TOPK, E])
        CHOSEN = sb("CHOSEN", [P, E], F32R)
        BEFORE = sb("BEFORE", [P, E], F32R)
        ONES = sb("ONES", [P, P], F32R)
        PLACE = sb("PLACE", [P, TOPK])
        FITS = sb("FITS", [P, TOPK])
        SLOTF = sb("SLOTF", [P, TOPK])
        SLOT = sb("SLOT", [P, TOPK], I32)

        s_wload = sem("wq_wo_gate_consts_loaded")
        s_first = sem("x_and_mask_of_batch_0_loaded")
        s_x0 = sem("x_loaded")
        s_mask = sem("mask_loaded")
        s_rowfill = sem("rows_filled")
        s_pre = sem("pool_prepared")
        s_tset = sem("setup_transposed")
        s_eset = sem("setup_copied")
        s_wqr = sem("wq_spread")
        s_xm0 = sem("x_of_batch_0_masked")
        s_xm = sem("x_masked")
        s_invc = sem("mask_subtracted")
        s_xi = sem("masked_x_ready")
        s_xs = sem("x_summed")
        s_svp = sem("masked_v_summed")
        s_sv = sem("masked_v_copied")
        s_invd = sem("mask_inverted")
        s_svl = sem("masked_v_split")
        s_cond = sem("condition_loaded")
        s_zero = sem("paddings_zeroed")
        s_vs = sem("v_staged")
        s_u = sem("pv_copied")
        s_ut = sem("pv_transposed")
        s_pj = sem("q_projected")
        s_vp = sem("v_projected")
        s_hi = sem("high_part_ready")
        s_ab = sem("q_operands_ready")
        s_xv = sem("xv_ready")
        s_ve = sem("v_ready")
        s_sc = sem("scores_ready")
        s_nm = sem("negmax_ready")
        s_nt = sem("negmax_transposed")
        s_nc = sem("negmax_copied")
        s_sh = sem("scores_shifted")
        s_ex = sem("exp_ready")
        s_pv = sem("pv_ready")
        s_ct = sem("context_ready")
        s_ctt = sem("context_transposed")
        s_ctc = sem("context_copied")
        s_wo = sem("out_projected")
        s_y = sem("y_copied")
        s_ytc = sem("yt_copied")
        s_xft = sem("xft_copied")
        s_lg = sem("logits_ready")
        s_top = sem("top_found")
        s_es = sem("router_exp_ready")
        s_ch = sem("choices_ready")
        s_ct2 = sem("choices_counted")
        s_lgc = sem("logits_copied")
        s_place = sem("places_ready")
        s_rs = sem("router_sum_inverted")
        s_slot = sem("slots_ready")
        s_scat = sem("rows_scattered")
        s_dve = sem("vector_in_order")
        s_pool = sem("pool_in_order")

        NG = 3
        GW_ = [min(P, SI - i * P) for i in range(NG)]
        CH = TOK // T
        SGS = [sb(f"SGS{i}", [P, T]) for i in range(2)]
        HS = sb("HS", [P, NG, T])

        s_sup = sem("shared_up_ready")
        s_ssg = sem("shared_silu_ready")
        s_hs = sem("shared_h_ready")
        s_sdn = sem("shared_down_ready")
        s_res = sem("residual_ready")

        B_PO, B_PJ, B_NM, B_FIN = 4, 5, 6, 7

        def scores(t2):
            return ps[:, 2 * t2:2 * t2 + 2, :]

        block = ctx.enter_context(nc.Block())

        @block.sync
        def _(sp):
            sp.dma_start(WQ[:], wq).then_inc(s_wload, 16)
            sp.dma_start(C[:], cst).then_inc(s_wload, 16)
            sp.dma_start(X[:, 0, :], x[0]).then_inc(s_first, 16)
            sp.dma_start(MASKB[:, 0, :], cond[0:1, :].broadcast_to([P, T])).then_inc(s_first, 16)
            sp.dma_start(WO[:], wo).then_inc(s_wload, 16)
            sp.dma_start(GW[:], gate_w).then_inc(s_wload, 16)
            sp.wait_ge(s_zero, 1)
            for n in range(2):
                sp.dma_start(COND[32 * n:32 * n + NB, :], cond).then_inc(s_cond, 16)
            sp.dma_start(CI[:], csti).then_inc(s_wload, 16)
            sp.dma_start(X[:, 1:NB, :], x[1:NB].rearrange("b p t -> p b t")).then_inc(s_x0, 16)
            sp.dma_start(MASKB[:, 1:NB, :].rearrange("p b t -> p (b t)"),
                         cond.rearrange("(a b) t -> a (b t)", a=1)[:, T:NB * T].broadcast_to([P, (NB - 1) * T])).then_inc(s_mask, 16)
            sp.wait_ge(s_pre, 1)
            for k in range(2):
                sp.dma_start(rows_dram[0:TRASH].rearrange("(e k p) c -> k p e c", k=2, p=P)[k],
                             FILL[:, k:k + 1, :].broadcast_to([P, E, ROW])).then_inc(s_rowfill, 16)
            for y in y_dram:
                sp.dma_start(y.rearrange("(n p) t -> p n t", p=P),
                             ZERO[:].unsqueeze(1).broadcast_to([P, YROWS // P, T])).then_inc(s_yzero, 16)
            for i, w in enumerate((sw1, sw3)):
                sp.dma_start(SW13[:, :, i, :], w.rearrange("(k p) n -> p k n", p=P)).then_inc(s_w, 16)
            for i in range(3):
                k = min(P, SI - i * P)
                sp.dma_start(SW2[0:k, i, :], sw2[i * P:i * P + k, :]).then_inc(s_w, 16)
            for e in range(4):
                load_expert(sp, e, e)
            sp.wait_ge(s_scat, 16 * TOPK * NB)
            for e in range(4):
                load_rows(sp, e, e)

        @block.gpsimd
        def _(po):
            nc.gpsimd.memset(COND[:], 0.0).then_inc(s_zero, 1)
            order = [0]

            def link(ins):
                order[0] += 1
                ins.then_inc(s_pool, 1)
                po.wait_ge(s_pool, order[0])

            link(nc.gpsimd.memset(ZERO[:], 0.0))
            link(nc.gpsimd.memset(FILL[:], 0.0))
            po.wait_ge(s_wload, 80)
            nc.gpsimd.tensor_copy(FILL[:, :, ROW - 1], CI[:, NB:NB + 2].bitcast(F32)).then_inc(s_pre, 1)
            nc.gpsimd.memset(ONES[:].bitcast(F32), 1.0)
            nc.gpsimd.memset(BEFORE[:].bitcast(F32), 0.0)
            po.wait_ge(s_x0, 16)
            po.wait_ge(s_mask, 16)
            nc.gpsimd.tensor_tensor(XM[:, 1:NB, :], X[:, 1:NB, :], MASKB[:, 1:NB, :], ALU.mult).then_inc(s_xm, 1)
            po.wait_ge(s_eset, 1)

            def values(b, used):
                po.wait_ge(s_vs, b + 1)
                if used:
                    po.wait_ge(s_pv, 2 * b)
                nc.gpsimd.tensor_copy(VP[:, :, :, DK], MASKT[:, :, bass.ds(b, 1)].broadcast_to([P, 2, NH]))
                nc.gpsimd.tensor_copy(VP[:, :, :, 0:DK].rearrange("p k h d -> p (k h) d"),
                                      VS[:, :, :, 0:DK].rearrange("p k h d -> p (k h) d")).then_inc(s_ve, 1)

            values(0, False)
            po.wait_ge(s_xm0, 1)
            po.wait_ge(s_xm, 1)
            nc.gpsimd.tensor_tensor(XI[:], X[:], XM[:], ALU.subtract).then_inc(s_xi, 1)
            po.wait_ge(s_invc, 1)
            nc.gpsimd.tensor_tensor(INVD[:], INVC[:].unsqueeze(1).broadcast_to([HL, NB, T]),
                                    C[0:HL, C_DIAG:C_DIAG + NB].unsqueeze(2).broadcast_to([HL, NB, T]), ALU.mult).then_inc(s_invd, 1)
            po.wait_ge(s_rowfill, 32)

            def scatter(b, used):
                if used:
                    po.wait_ge(s_scat, 16 * TOPK * b)
                nc.gpsimd.tensor_copy(PAY[:, ROW - 1:ROW], CI[:, bass.ds(b, 1)].bitcast(F32)).then_inc(s_slot, 1)
                wait_apart(po, s_place, b + 1, s_rowfill, 32)
                nc.gpsimd.tensor_scalar(FITS[:], PLACE[:], float(CAP), None, ALU.is_lt).then_inc(s_slot, 1)
                nc.gpsimd.tensor_scalar(SLOTF[:], TOPF[:, 0:TOPK], float(CAP), C[:, C_TRASH:C_TRASH + 1],
                                        ALU.mult, ALU.subtract).then_inc(s_slot, 1)
                wait_apart(po, s_slot, 7 * b + 3, s_rowfill, 32)
                nc.gpsimd.tensor_tensor(SLOTF[:], SLOTF[:], PLACE[:], ALU.add).then_inc(s_slot, 1)
                wait_apart(po, s_slot, 7 * b + 4, s_rowfill, 32)
                nc.gpsimd.tensor_tensor(SLOTF[:], SLOTF[:], FITS[:], ALU.mult).then_inc(s_slot, 1)
                wait_apart(po, s_slot, 7 * b + 5, s_rowfill, 32)
                nc.gpsimd.tensor_scalar(SLOT[:], SLOTF[:], C[:, C_TRASH:C_TRASH + 1], None, ALU.add).then_inc(s_slot, 1)
                wait_apart(po, s_rs, b + 1, s_rowfill, 32)
                nc.gpsimd.tensor_scalar(PAY[:, T:T + E], ES[:], RSUM[:, 0:1], None, ALU.mult).then_inc(s_slot, 1)
                wait_apart(po, s_slot, 7 * b + 7, s_rowfill, 32)
                for k in range(TOPK):
                    po.indirect_dma_start(out=rows_dram, out_offset=bass.IndirectOffsetOnAxis(ap=SLOT[:, k:k + 1], axis=0),
                                          in_=PAY[:], in_offset=None).then_inc(s_scat, 16)

            values(1, True)
            values(2, True)
            scatter(0, False)
            with po.Fori(3, NB - 1) as b:
                values(b, True)
                scatter(b - 2, True)
            values(NB - 1, True)
            scatter(NB - 3, True)
            scatter(NB - 2, True)
            scatter(NB - 1, True)
            po.wait_ge(s_scat, 16 * TOPK * NB)

        @block.tensor
        def _(pe):
            pe.wait_ge(s_wload, 80)
            pe.wait_ge(s_cond, 32)
            nc.tensor.transpose(ps[:, B_PJ, 0:P], WQ[:], IDENT)
            for k in range(2):
                nc.tensor.transpose(ps[:, B_PJ, P + k * E:P + (k + 1) * E], GW[:, k * P:(k + 1) * P], C[0:E, C_ID:C_ID + E])
            for k in range(2):
                nc.tensor.transpose(ps[:, B_PJ, 192 + k * NB:192 + (k + 1) * NB], COND[0:NB, k * P:(k + 1) * P],
                                    C[0:NB, C_ID:C_ID + NB])
            nc.tensor.transpose(ps[:, B_PJ, 256:256 + P], WO[:], IDENT).then_inc(s_tset, 1)

            def project(b, half):
                for i in range(2):
                    ins = nc.tensor.matmul(ps[:, B_PJ, i * T:(i + 1) * T],
                                           WQR[:, 2 * half + i].rearrange("p h r d -> p (h r d)"),
                                           XM[:, bass.ds(b, 1), :].rearrange("p a t -> p (a t)"), start=True, stop=True)
                ins.then_inc(s_pj, 1)

            def project_v(b):
                pe.wait_ge(s_xv, b + 1)
                for k in range(2):
                    ins = nc.tensor.matmul(ps[:, B_PJ, k * P:(k + 1) * P], XV[:, k * P:(k + 1) * P], WQT[:],
                                           start=True, stop=True)
                ins.then_inc(s_vp, 1)

            def score(b, j, free):
                if free:
                    pe.wait_ge(s_ex, 4 * b + j - 1)
                if j in (0, 2):
                    pe.wait_ge(s_ab, 2 * b + 1 + j // 2)
                for hh in range(2):
                    for k in range(2):
                        ins = nc.tensor.matmul(scores(j % 2)[:, hh, k * T:(k + 1) * T],
                                               QA[64 * hh:64 * hh + 64, j, k * P:(k + 1) * P],
                                               QB[64 * hh:64 * hh + 64, j, :], start=(k == 0), stop=False,
                                               skip_group_check=True)
                ins.then_inc(s_sc, 1)

            def shift(b, j):
                pe.wait_ge(s_nc, 4 * b + j + 1)
                for hh in range(2):
                    for q in range(2):
                        ins = nc.tensor.matmul(
                            scores(j % 2)[:, hh, :].rearrange("p (k t) -> p k t", k=2)[:, :, q * P:(q + 1) * P], SEL[:, q, hh, :],
                            NMT[:].unsqueeze(1).broadcast_to([8, 2, P]), start=False, stop=True, skip_group_check=True)
                ins.then_inc(s_sh, 1)

            def weigh(b, g, po_used):
                pe.wait_ge(s_ex, 4 * b + 2 * g + 2)
                if g == 0:
                    pe.wait_ge(s_ve, b + 1)
                    if po_used:
                        pe.wait_ge(s_u, b)
                    for n in range(2):
                        nc.tensor.matmul(ps[:, B_PO, n * T:(n + 1) * T], SV[:, n].rearrange("p i d -> p (i d)"),
                                         INVD[:, bass.ds(b, 1), :].rearrange("p a n -> p (a n)"),
                                         start=(n == 0), stop=False, skip_group_check=True)
                for k in range(2):
                    for i in range(4):
                        h = 4 * g + i
                        ins = nc.tensor.matmul(ps[32 * i:32 * i + DV, B_PO, g * T:(g + 1) * T], VP[:, k, h, :],
                                               EX[:, h // 2, h % 2, k, :], start=False, stop=(k == 1),
                                               skip_group_check=True)
                ins.then_inc(s_pv, 1)

            def turn_max(b, j):
                pe.wait_ge(s_nm, 4 * b + j + 1)
                nc.tensor.transpose(ps[0:8, B_NM, 0:P], NM2[:].rearrange("p k r h -> p (k r h)"), IDENT).then_inc(s_nt, 1)

            def turn_sums(b, used):
                if used:
                    pe.wait_ge(s_place, b)
                pe.wait_ge(s_u, b + 1)
                for q in range(2):
                    for g in range(2):
                        ins = nc.tensor.transpose(ps[:, B_FIN, (2 * q + g) * P:(2 * q + g + 1) * P], U[:, g, q * P:(q + 1) * P], IDENT)
                ins.then_inc(s_ut, 1)

            def turn_context(b):
                pe.wait_ge(s_ct, b + 1)
                for q in range(2):
                    ins = nc.tensor.transpose(ps[:, B_FIN, q * P:(q + 1) * P], CTX[:, q, :], IDENT)
                ins.then_inc(s_ctt, 1)

            def out_project(b):
                pe.wait_ge(s_ctc, b + 1)
                for k in range(2):
                    ins = nc.tensor.matmul(ps[:, B_FIN, T + k * P:T + (k + 1) * P], CTT[:, k * P:(k + 1) * P], WOT[:],
                                           start=True, stop=True)
                ins.then_inc(s_wo, 1)

            def logits(b):
                pe.wait_ge(s_xft, b + 1)
                for k in range(2):
                    ins = nc.tensor.transpose(ps[:, B_FIN, E + k * P:E + (k + 1) * P], YT[:, k, :], IDENT)
                for k in range(2):
                    ins = nc.tensor.matmul(ps[:, B_FIN, 0:E], YT[:, k, :], GWT[:, k, :], start=(k == 0), stop=(k == 1))
                ins.then_inc(s_lg, 1)

            def count(b):
                pe.wait_ge(s_ch, b + 1)
                pe.wait_ge(s_y, b + 1)
                nc.tensor.matmul(ps[:, B_FIN, 0:E], UP[:], CHOSEN[:], start=True, stop=False)
                nc.tensor.matmul(ps[:, B_FIN, 0:E], ONES[:], BEFORE[:], start=False, stop=True).then_inc(s_ct2, 1)

            def step(b, j, has_prev, has_prev2, has_next, first=False):
                if j < 3:
                    score(b, j + 1, has_prev or j > 0)
                elif has_next:
                    score(b + 1, 0, True)
                shift(b, j)
                if j == 0 and has_prev2:
                    logits(b - 2)
                if j == 3 and has_prev:
                    turn_context(b - 1)
                if not has_prev and j == 1:
                    pe.wait_ge(s_xs, 1)
                    nc.tensor.matmul(ps[0:HL, B_FIN, 0:P], XS[:], WQT[:], start=True, stop=True).then_inc(s_svp, 1)
                if not has_prev and j == 2:
                    pe.wait_ge(s_svl, 1)
                    pe.wait_ge(s_invd, 1)
                if j == 2:
                    weigh(b, 0, has_prev)
                if j == 0 and has_prev:
                    weigh(b - 1, 1, True)
                if j == 0 and has_next:
                    pe.wait_ge(s_ab, 2 * b + 2)
                    project_v(b + 1)
                if j == 1:
                    if has_prev2:
                        count(b - 2)
                    if has_next:
                        pe.wait_ge(s_vs, b + 2)
                        project(b + 1, 0)
                if j == 2 and has_prev:
                    turn_sums(b - 1, has_prev2)
                if j == 3:
                    if has_next:
                        pe.wait_ge(s_ab, 2 * b + 3)
                        project(b + 1, 1)
                    if has_prev:
                        out_project(b - 1)
                if j < 3:
                    turn_max(b, j + 1)
                elif has_next:
                    turn_max(b + 1, 0)

            pe.wait_ge(s_wqr, 3)
            pe.wait_ge(s_xm0, 1)
            project(0, 0)
            pe.wait_ge(s_ab, 1)
            project(0, 1)
            pe.wait_ge(s_eset, 2)
            score(0, 0, False)
            turn_max(0, 0)
            pe.wait_ge(s_ab, 2)
            project_v(0)
            for j in range(4):
                step(0, j, False, False, True, first=True)
            for j in range(4):
                step(1, j, True, False, True)
            for j in range(4):
                step(2, j, True, True, True, first=True)
            with pe.Fori(3, NB - 1) as b:
                for j in range(4):
                    step(b, j, True, True, True)
            for j in range(4):
                step(NB - 1, j, True, True, False)

            def shared_up(c, i):
                if NG * c + i >= 2:
                    pe.wait_ge(s_hs, NG * c + i - 1)
                for u in range(2):
                    for k in range(2):
                        ins = nc.tensor.matmul(ps[0:GW_[i], 2 * ((NG * c + i) % 2) + u, 0:T], SW13[:, k, u, i * P:i * P + GW_[i]],
                                               XFT[:, k, c * T:(c + 1) * T], start=(k == 0), stop=(k == 1))
                ins.then_inc(s_sup, 1)

            def shared_down(c):
                pe.wait_ge(s_hs, NG * c + NG)
                if c:
                    pe.wait_ge(s_res, c)
                for st in range(2):
                    for i in range(NG):
                        ins = nc.tensor.matmul(ps[:, B_PJ, st * T:(st + 1) * T], HS[0:GW_[i], i, st * P:(st + 1) * P],
                                               SW2[0:GW_[i], i, :], start=(i == 0), stop=(i == NG - 1))
                ins.then_inc(s_sdn, 1)

            weigh(NB - 1, 1, True)
            logits(NB - 2)
            pe.wait_ge(s_w, 80)
            shared_up(0, 0)
            shared_up(0, 1)
            count(NB - 2)
            shared_up(0, 2)
            turn_sums(NB - 1, True)
            shared_down(0)
            shared_up(1, 0)
            turn_context(NB - 1)
            shared_up(1, 1)
            out_project(NB - 1)
            shared_up(1, 2)
            logits(NB - 1)
            shared_down(1)
            shared_up(2, 0)
            count(NB - 1)
            shared_up(2, 1)
            shared_up(2, 2)
            shared_down(2)
            for i in range(NG):
                shared_up(3, i)
            shared_down(3)

        @block.scalar
        def _(act):
            act.wait_ge(s_tset, 1)
            nc.scalar.activation(WQT[:], ps[:, B_PJ, 0:P], ACT.Copy).then_inc(s_wqr, 1)
            nc.scalar.activation(MASKT[:].rearrange("p k b -> p (k b)"), ps[:, B_PJ, 192:192 + 2 * NB], ACT.Copy).then_inc(s_eset, 1)
            nc.scalar.activation(GWT[:].rearrange("p k b -> p (k b)"), ps[:, B_PJ, P:P + 2 * E], ACT.Copy)
            nc.scalar.activation(WOT[:], ps[:, B_PJ, 256:256 + P], ACT.Copy).then_inc(s_wqr, 1)
            nc.scalar.activation(UP[:], C[:, C_UP:C_UP + P], ACT.Copy)
            nc.scalar.activation(SEL[:].rearrange("p q h n -> p (q h n)"), C[0:8, C_SEL:C_SEL + 4 * P], ACT.Copy).then_inc(s_eset, 1)

            def high(b, half, first=False):
                act.wait_ge(s_pj, 2 * b + 1 + half)
                if not first:
                    act.wait_ge(s_ab, 2 * b + half)
                nc.scalar.activation(HI[:].rearrange("p i t -> p (i t)"), ps[:, B_PJ, :], ACT.Copy).then_inc(s_hi, 1)

            def negmax(b, j):
                act.wait_ge(s_nt, 4 * b + j + 1)
                nc.scalar.activation(NMT[:], ps[0:8, B_NM, 0:P], ACT.Copy).then_inc(s_nc, 1)

            def exps(b, j, used):
                act.wait_ge(s_sh, 4 * b + j + 1)
                if used:
                    act.wait_ge(s_pv, 2 * b - 1 + j // 2)
                nc.scalar.activation(EX[:, j].rearrange("p h k t -> p h (k t)"), scores(j % 2), ACT.Exp,
                                     scale=float(DK) ** -0.5).then_inc(s_ex, 1)

            def turned_x(b):
                act.wait_ge(s_vp, b)
                nc.scalar.activation(XV[:], XM[:, bass.ds(b, 1), :].rearrange("p a t -> p (a t)"), ACT.Copy).then_inc(s_xv, 1)

            def masked_sums():
                act.wait_ge(s_svp, 1)
                nc.scalar.activation(SV[:, :, :, 0:DK].rearrange("p g i d -> p (g i) d"),
                                     ps[0:HL, B_FIN, 0:P].rearrange("p (h d) -> p h d", h=NH), ACT.Copy).then_inc(s_sv, 1)

            def values(b, used=True):
                act.wait_ge(s_vp, b + 1)
                if used:
                    act.wait_ge(s_ve, b)
                nc.scalar.activation(VS[:, :, :, 0:DK].rearrange("p k h d -> p (k h) d"),
                                     ps[:, B_PJ, 0:2 * P].rearrange("p (k h d) -> p (k h) d", k=2, h=NH),
                                     ACT.Copy).then_inc(s_vs, 1)

            def keep_sums(b, used):
                act.wait_ge(s_pv, 2 * b + 2)
                if used:
                    act.wait_ge(s_ut, b)
                nc.scalar.activation(U[:].rearrange("p g t -> p (g t)"), ps[:, B_PO, :], ACT.Copy).then_inc(s_u, 1)

            def keep_context(b):
                act.wait_ge(s_ctt, b + 1)
                nc.scalar.activation(CTT[:], ps[:, B_FIN, 0:T], ACT.Copy).then_inc(s_ctc, 1)

            def keep_y(b, used):
                act.wait_ge(s_wo, b + 1)
                nc.scalar.activation(YT[:].rearrange("p k n -> p (k n)"), ps[:, B_FIN, T:2 * T], ACT.Copy).then_inc(s_ytc, 1)
                nc.scalar.activation(XFT[:, :, bass.ds(b * P, P)], ps[:, B_FIN, T:2 * T].rearrange("p (k n) -> p k n", k=2),
                                     ACT.Copy).then_inc(s_xft, 1)

            def keep_logits(b, used):
                act.wait_ge(s_lg, b + 1)
                if used:
                    act.wait_ge(s_ch, b)
                nc.scalar.activation(LG[:], ps[:, B_FIN, 0:E], ACT.Copy).then_inc(s_lgc, 1)
                if used:
                    act.wait_ge(s_scat, 16 * TOPK * b)
                nc.scalar.activation(PAY[:, 0:T], ps[:, B_FIN, E:E + T], ACT.Copy).then_inc(s_y, 1)

            def router_exp(b, used):
                act.wait_ge(s_top, b + 1)
                if used:
                    act.wait_ge(s_slot, 7 * b)
                nc.scalar.activation(ES[:], LG[:], ACT.Exp, bias=NTOP[:], accum_out=ESUM[:]).then_inc(s_es, 1)

            def step(b, j, has_prev, has_prev2, has_next, first=False):
                if j == 0 and has_next:
                    turned_x(b + 1)
                if j == 1 and has_next:
                    values(b + 1)
                if j == 3 and has_prev:
                    keep_context(b - 1)
                exps(b, j, has_prev)
                if j == 0 and has_prev:
                    keep_sums(b - 1, has_prev2)
                if j == 0 and has_prev2:
                    keep_logits(b - 2, not first)
                if j == 1 and has_next:
                    high(b + 1, 0)
                if j == 3 and has_next:
                    high(b + 1, 1)
                if j < 3:
                    negmax(b, j + 1)
                elif has_next:
                    negmax(b + 1, 0)
                if j == 0 and has_prev2:
                    router_exp(b - 2, not first)
                if j == 3 and has_prev:
                    keep_y(b - 1, has_prev2)
                if j == 1 and not has_prev:
                    masked_sums()

            high(0, 0, True)
            high(0, 1)
            negmax(0, 0)
            values(0, False)
            act.wait_ge(s_xm, 1)
            for j in range(4):
                step(0, j, False, False, True, first=True)
            for j in range(4):
                step(1, j, True, False, True)
            for j in range(4):
                step(2, j, True, True, True, first=True)
            with act.Fori(3, NB - 1) as b:
                for j in range(4):
                    step(b, j, True, True, True)
            for j in range(4):
                step(NB - 1, j, True, True, False)

            def shared_silu(c, i):
                t = NG * c + i
                act.wait_ge(s_sup, t + 1)
                if t >= 2:
                    act.wait_ge(s_hs, t - 1)
                nc.scalar.activation(SGS[t % 2][0:GW_[i], :], ps[0:GW_[i], 2 * (t % 2), 0:T], ACT.Silu).then_inc(s_ssg, 1)

            keep_sums(NB - 1, True)
            keep_logits(NB - 2, True)
            router_exp(NB - 2, True)
            shared_silu(0, 0)
            shared_silu(0, 1)
            shared_silu(0, 2)
            shared_silu(1, 0)
            keep_context(NB - 1)
            shared_silu(1, 1)
            keep_y(NB - 1, True)
            shared_silu(1, 2)
            keep_logits(NB - 1, True)
            router_exp(NB - 1, True)
            for c in (2, 3):
                for i in range(NG):
                    shared_silu(c, i)

        @block.vector
        def _(dve):
            state = {"base": 0, "k": 0}

            def link(ins, apart=False):
                state["k"] += 1
                ins.then_inc(s_dve, 1)
                if apart:
                    wait_apart(dve, s_dve, state["base"] + state["k"], s_mask, 16)
                else:
                    dve.wait_ge(s_dve, state["base"] + state["k"])

            dve.wait_ge(s_first, 32)
            nc.vector.tensor_tensor(XM[:, 0, :], X[:, 0, :], MASKB[:, 0, :], ALU.mult).then_inc(s_xm0, 1)
            dve.wait_ge(s_xm0, 1)
            nc.vector.tensor_copy(XV[:], XM[:, 0, :]).then_inc(s_xv, 1)
            dve.wait_ge(s_wqr, 1)
            nc.vector.tensor_copy(WQR[:].rearrange("p j h r d -> p (j h) r d"),
                                  WQT[:].rearrange("p (h d) -> p h d", h=NH).unsqueeze(2).broadcast_to([P, NH, 4, DK])
                                  ).then_inc(s_wqr, 1)

            def operands(b, half, used):
                dve.wait_ge(s_hi, 2 * b + 1 + half)
                if used:
                    dve.wait_ge(s_sc, 4 * b - 2 + 2 * half)
                q = ps[:, B_PJ, :].rearrange("p (i t) -> p i t", i=2)
                for n, dst in enumerate((QA, QB)):
                    ins = nc.vector.scalar_tensor_tensor(
                        out=dst[:, 2 * half:2 * half + 2, :], in0=HI[:].bitcast(F32),
                        scalar=C[:, C_SPLIT + n:C_SPLIT + n + 1], in1=q, op0=ALU.mult, op1=ALU.add)
                ins.then_inc(s_ab, 1)

            def negmax(b, j, used):
                dve.wait_ge(s_sc, 4 * b + j + 1)
                link(nc.vector.tensor_reduce(NEGMAX[:], scores(j % 2).rearrange("p h (k t) -> p h k t", k=2),
                                             AX.X, ALU.max, negate=True))
                nm = NEGMAX[:].rearrange("p h k -> p k h")
                if used:
                    dve.wait_ge(s_nt, 4 * b + j)
                link(nc.vector.tensor_copy(NM2[:, :, 0, :].bitcast(F32R), nm))
                nc.vector.tensor_tensor(NM2[:, :, 1, :], nm, NM2[:, :, 0, :], ALU.subtract).then_inc(s_nm, 1)

            def context(b, used):
                dve.wait_ge(s_ut, b + 1)
                sums = ps[:, B_FIN, :].rearrange("p (n d) -> p n d", d=32)
                link(nc.vector.reciprocal(RDEN[:], sums[:, :, DK:DV]))
                if used:
                    dve.wait_ge(s_ctt, b)
                nc.vector.tensor_tensor(CTX[:].rearrange("p q (h d) -> p (q h) d", d=DK), sums[:, :, 0:DK],
                                        RDEN[:].broadcast_to([P, 2 * NH, DK]), ALU.mult).then_inc(s_ct, 1)

            def choose(b, used):
                if used:
                    dve.wait_ge(s_slot, 7 * b)
                wait_apart(dve, s_lgc, b + 1, s_mask, 16)
                link(nc.vector.max(TOP[:], LG[:]))
                nc.vector.tensor_scalar(NTOP[:], TOP[:, 0:1], -1.0, None, ALU.mult).then_inc(s_top, 1)
                link(nc.vector.max_index(TOPI[:], TOP[:], LG[:]))
                link(nc.vector.tensor_copy(TOPF[:], TOPI[:]))
                link(nc.vector.tensor_tensor(ONEH[:], C[:, C_IOTA:C_IOTA + E].unsqueeze(1).broadcast_to([P, TOPK, E]),
                                             TOPF[:, 0:TOPK].unsqueeze(2).broadcast_to([P, TOPK, E]), ALU.is_equal))
                with nc.allow_low_precision(reason="zeros and ones"):
                    nc.vector.tensor_reduce(CHOSEN[:], ONEH[:].rearrange("p k e -> p e k"), AX.X, ALU.add).then_inc(s_ch, 1)

            def place(b):
                dve.wait_ge(s_ct2, b + 1)
                link(nc.vector.tensor_tensor(PICK[:], ONEH[:], ps[:, B_FIN, 0:E].unsqueeze(1).broadcast_to([P, TOPK, E]),
                                             ALU.mult))
                nc.vector.tensor_tensor(BEFORE[:], BEFORE[:].bitcast(F32), CHOSEN[:].bitcast(F32), ALU.add)
                nc.vector.tensor_reduce(PLACE[:], PICK[:], AX.X, ALU.add).then_inc(s_place, 1)
                dve.wait_ge(s_es, b + 1)
                nc.vector.reciprocal(RSUM[:], ESUM[:]).then_inc(s_rs, 1)

            def x_sums():
                dve.wait_ge(s_xi, 1)
                link(nc.vector.tensor_reduce(XS[:, 0:NB], XI[:], AX.X, ALU.add))
                nc.vector.tensor_copy(XS[:, 32:HL], XS[:, 0:NB]).then_inc(s_xs, 1)

            def low_sums():
                dve.wait_ge(s_sv, 1)
                low = SV[32:HL, :, :, 0:DK].rearrange("p g i d -> p (g i) d")
                nc.vector.tensor_tensor(low, ps[32:HL, B_FIN, 0:P].rearrange("p (h d) -> p h d", h=NH), low.bitcast(F32),
                                        ALU.subtract).then_inc(s_svl, 1)

            def step(b, j, has_prev, has_prev2, has_next, first=False):
                if j < 3:
                    negmax(b, j + 1, True)
                elif has_next:
                    negmax(b + 1, 0, True)
                if j == 0 and not has_prev:
                    x_sums()
                if j == 1 and not has_prev:
                    low_sums()
                if j == 0 and has_prev2:
                    choose(b - 2, not first)
                if j == 1 and has_prev2:
                    place(b - 2)
                if j == 1 and has_next:
                    operands(b + 1, 0, True)
                if j == 2 and has_prev:
                    context(b - 1, has_prev2)
                if j == 3 and has_next:
                    operands(b + 1, 1, True)

            dve.wait_ge(s_cond, 32)
            link(nc.vector.tensor_scalar(INVC[:], COND[:], -1.0, 1.0, ALU.mult, ALU.add))
            link(nc.vector.memset(SV[:].bitcast(F32), 0.0))
            link(nc.vector.memset(XS[:], 0.0))
            link(nc.vector.tensor_reduce(MASKED[:], INVC[0:NB, :], AX.X, ALU.add))
            nc.vector.tensor_copy(SV[0:NB, :, :, DK:DV].rearrange("p g i d -> p (g i) d"),
                                  MASKED[:].unsqueeze(1).broadcast_to([NB, NH, 1])).then_inc(s_invc, 1)
            operands(0, 0, False)
            operands(0, 1, False)
            negmax(0, 0, False)
            for j in range(4):
                step(0, j, False, False, True, first=True)
            for j in range(4):
                step(1, j, True, False, True)
            for j in range(4):
                step(2, j, True, True, True, first=True)
            base, per = state["k"], PER_BATCH
            with dve.Fori(3, NB - 1) as b:
                state["base"], state["k"] = base + (b - 3) * per, 0
                for j in range(4):
                    step(b, j, True, True, True)
                assert state["k"] == per, state["k"]
            state["base"], state["k"] = base + (NB - 4) * per, 0
            for j in range(4):
                step(NB - 1, j, True, True, False)

            def shared_hidden(c, i):
                t = NG * c + i
                dve.wait_ge(s_ssg, t + 1)
                if c and i == 0:
                    dve.wait_ge(s_sdn, c)
                nc.vector.tensor_tensor(HS[0:GW_[i], i, :], SGS[t % 2][0:GW_[i], :], ps[0:GW_[i], 2 * (t % 2) + 1, 0:T],
                                        ALU.mult).then_inc(s_hs, 1)

            def shared_add(c):
                dve.wait_ge(s_sdn, c + 1)
                xc = X[:, 2 * c:2 * c + 2, :]
                nc.vector.tensor_tensor(xc, xc, ps[:, B_PJ, :].rearrange("p (s t) -> p s t", s=2), ALU.add).then_inc(s_res, 1)

            choose(NB - 2, True)
            shared_hidden(0, 0)
            shared_hidden(0, 1)
            place(NB - 2)
            shared_hidden(0, 2)
            context(NB - 1, True)
            shared_add(0)
            for i in range(NG):
                shared_hidden(1, i)
            choose(NB - 1, True)
            shared_add(1)
            shared_hidden(2, 0)
            place(NB - 1)
            shared_hidden(2, 1)
            shared_hidden(2, 2)
            shared_add(2)
            for i in range(NG):
                shared_hidden(3, i)
            shared_add(3)


PER_BATCH = 14


def experts(nc, sb, sem, ps, y_dram, X, XB, W1, W3, W2A, W2B, IDENT, s_ew, s_xb, s_yzero,
            load_expert, load_rows, out):
    TAIL = INTER - HEADW
    with ExitStack() as ctx:
        def sb(name, shape, dt=F32):
            return ctx.enter_context(nc.sbuf_tensor(name, shape, dt))

        RING = len(W1)
        META = [sb(f"META{i}", [P, 2, 2]) for i in range(RING)]
        XT = [sb(f"XT{i}", [P, 2, CAP]) for i in range(2)]
        SG = [sb(f"SG{i}", [P, 2, CAP]) for i in range(2)]
        HA = [sb(f"HA{i}", [P, CAP]) for i in range(2)]
        HB = [sb(f"HB{i}", [TAIL, CAP]) for i in range(2)]
        O = [sb(f"O{i}", [P, 2, T]) for i in range(RING)]
        YS = sb("YS", [P, 2, NB, T])

        s_tr = sem("rows_transposed")
        s_xt = sem("xt_ready")
        s_meta = sem("meta_ready")
        s_up = sem("up_ready")
        s_sg = sem("silu_ready")
        s_h = sem("h_ready")
        s_dn = sem("down_ready")
        s_o = sem("weighted_ready")
        s_acc = [sem(f"results_added{i}") for i in range(2)]
        s_yl = sem("y_loaded")
        s_fin = sem("final_ready")
        s_final_chain = sem("y_halves_added")
        s_out = sem("stored")

        B_UP, B_T, B_DN = 0, 4, 6

        block = ctx.enter_context(nc.Block())

        @block.sync
        def _(sp):
            with sp.Fori(0, (E - 4) // 4) as i:
                for m in range(4):
                    sp.wait_ge(s_meta, 4 * i + m + 1)
                    sp.wait_ge(s_tr, 4 * i + m + 1)
                    load_rows(sp, 4 * i + m + 4, m)
                    sp.wait_ge(s_dn, 4 * i + m + 1)
                    load_expert(sp, 4 * i + m + 4, m)
            for par in range(2):
                sp.wait_ge(s_acc[par], 16 * E)
            for n in range(2):
                sp.dma_start(YS[:, n], y_dram[n][0:TOK].rearrange("(b p) t -> p b t", p=P)).then_inc(s_yl, 16)
            for n in range(2):
                sp.wait_ge(s_fin, n + 1)
                h = NB // 2
                sp.dma_start(out[n * h:(n + 1) * h].rearrange("b p t -> p b t"), X[:, n * h:(n + 1) * h, :]).then_inc(s_out, 16)
            sp.wait_ge(s_out, 32)

        @block.gpsimd
        def _(po):
            po.wait_ge(s_yzero, 32)
            def add(e, m, par, used):
                if used:
                    wait_apart(po, s_acc[par], 16 * (e - m) + 32 * (m // 2), s_yzero, 32)
                wait_apart(po, s_o, e + 1, s_yzero, 32)
                for k in range(2):
                    po.indirect_dma_start(out=y_dram[par], out_offset=bass.IndirectOffsetOnAxis(
                        ap=META[m][:, k, 1:2].bitcast(I32), axis=0), in_=O[m][:, k, :], in_offset=None,
                        compute_op=ALU.add).then_inc(s_acc[par], 16)

            for e in range(4):
                add(e, e, e % 2, e >= 2)
            with po.Fori(1, E // 4) as i:
                for m in range(4):
                    add(4 * i + m, m, m % 2, True)
            for par in range(2):
                po.wait_ge(s_acc[par], 16 * E)

        @block.tensor
        def _(pe):
            def turn(e, m, free):
                pe.wait_ge(s_xb[m], 16 * (e // 4) + 16 if isinstance(e, int) else (e - m) * 4 + 16)
                if free:
                    pe.wait_ge(s_xt, e - 1)
                for st in range(2):
                    for k in range(2):
                        ins = nc.tensor.transpose(ps[:, B_T + m % 2, k * CAP + st * P:k * CAP + (st + 1) * P],
                                                  XB[m][:, st, k * P:(k + 1) * P], IDENT)
                ins.then_inc(s_tr, 1)

            def up(e, m, free):
                pe.wait_ge(s_ew[m], 80 * (e // 4) + 80 if isinstance(e, int) else (e - m) * 20 + 80)
                pe.wait_ge(s_xt, e + 1)
                if free:
                    pe.wait_ge(s_h, e - 1)
                b0 = B_UP + 2 * (m % 2)
                for lhs, dst in ((lambda k: W1[m][:, k, 0:P], ps[:, b0, 0:CAP]),
                                 (lambda k: W1[m][:, k, HEADW:INTER + TAIL], ps[:, b0, CAP:2 * CAP]),
                                 (lambda k: W3[m][:, k, 0:P], ps[:, b0 + 1, 0:CAP])):
                    for k in range(2):
                        ins = nc.tensor.matmul(dst, lhs(k), XT[m % 2][:, k, :], start=(k == 0), stop=(k == 1))
                ins.then_inc(s_up, 1)

            def down(e, m, free):
                pe.wait_ge(s_h, e + 1)
                if free:
                    pe.wait_ge(s_o, e - 1)
                for st in range(2):
                    cols = slice(st * P, (st + 1) * P)
                    dst = ps[:, B_DN + m % 2, st * T:(st + 1) * T]
                    nc.tensor.matmul(dst, HA[m % 2][0:HEADW, cols], W2A[m][:], start=True, stop=False)
                    ins = nc.tensor.matmul(dst, HB[m % 2][:, cols], W2B[m][:], start=False, stop=True)
                ins.then_inc(s_dn, 1)

            turn(0, 0, False)
            turn(1, 1, False)
            up(0, 0, False)
            turn(2, 2, True)
            up(1, 1, False)
            down(0, 0, False)
            turn(3, 3, True)
            up(2, 2, True)
            down(1, 1, False)
            with pe.Fori(0, (E - 4) // 4) as i:
                for m in range(4):
                    turn(4 * i + m + 4, m, True)
                    up(4 * i + m + 3, (m + 3) % 4, True)
                    down(4 * i + m + 2, (m + 2) % 4, True)
            up(E - 1, 3, True)
            down(E - 2, 2, True)
            down(E - 1, 3, True)

        @block.scalar
        def _(act):
            def rows(e, m, used):
                act.wait_ge(s_tr, e + 1)
                if used:
                    act.wait_ge(s_up, e - 1)
                nc.scalar.activation(XT[m % 2][:].rearrange("p k n -> p (k n)"), ps[:, B_T + m % 2, :], ACT.Copy).then_inc(s_xt, 1)

            def silu(e, m, used):
                act.wait_ge(s_up, e + 1)
                if used:
                    act.wait_ge(s_h, e - 1)
                nc.scalar.activation(SG[m % 2][:].rearrange("p k n -> p (k n)"), ps[:, B_UP + 2 * (m % 2), :], ACT.Silu).then_inc(s_sg, 1)

            rows(0, 0, False)
            rows(1, 1, False)
            silu(0, 0, False)
            rows(2, 2, True)
            silu(1, 1, False)
            rows(3, 3, True)
            silu(2, 2, True)
            with act.Fori(0, (E - 4) // 4) as i:
                for m in range(4):
                    rows(4 * i + m + 4, m, True)
                    silu(4 * i + m + 3, (m + 3) % 4, True)
            silu(E - 1, 3, True)

        @block.vector
        def _(dve):
            def meta(e, m, used):
                dve.wait_ge(s_xb[m], 16 * (e // 4) + 16 if isinstance(e, int) else (e - m) * 4 + 16)
                if used:
                    dve.wait_ge(s_acc[m % 2], 16 * (e - m) - 32 + 32 * (m // 2))
                nc.vector.tensor_copy(META[m][:, :, 1:2], XB[m][:, :, ROW - 1:ROW])
                nc.vector.tensor_copy(META[m][:, :, 0:1], XB[m][:, :, bass.ds(e + T, 1)]).then_inc(s_meta, 1)

            def hidden(e, m):
                dve.wait_ge(s_sg, e + 1)
                b0 = B_UP + 2 * (m % 2)
                nc.vector.tensor_tensor(HA[m % 2][:], SG[m % 2][:, 0, :], ps[:, b0 + 1, 0:CAP], ALU.mult)
                nc.vector.tensor_tensor(HB[m % 2][:], SG[m % 2][0:TAIL, 1, :], ps[64:64 + TAIL, b0, CAP:2 * CAP],
                                        ALU.mult).then_inc(s_h, 1)

            def weighted(e, m):
                dve.wait_ge(s_dn, e + 1)
                dve.wait_ge(s_meta, e + 1)
                for st in range(2):
                    ins = nc.vector.tensor_scalar(O[m][:, st, :], ps[:, B_DN + m % 2, st * T:(st + 1) * T],
                                                  META[m][:, st, 0:1], None, ALU.mult)
                ins.then_inc(s_o, 1)

            meta(0, 0, False)
            meta(1, 1, False)
            hidden(0, 0)
            meta(2, 2, False)
            hidden(1, 1)
            weighted(0, 0)
            meta(3, 3, False)
            hidden(2, 2)
            weighted(1, 1)
            with dve.Fori(0, (E - 4) // 4) as i:
                for m in range(4):
                    hidden(4 * i + m + 3, (m + 3) % 4)
                    weighted(4 * i + m + 2, (m + 2) % 4)
                    meta(4 * i + m + 4, m, True)
            hidden(E - 1, 3)
            weighted(E - 2, 2)
            weighted(E - 1, 3)
            dve.wait_ge(s_yl, 32)
            h = NB // 2
            for n in range(2):
                half = slice(n * h, (n + 1) * h)
                nc.vector.tensor_tensor(YS[:, 0, half, :], YS[:, 0, half, :], YS[:, 1, half, :], ALU.add).then_inc(s_final_chain, 1)
                dve.wait_ge(s_final_chain, n + 1)
                nc.vector.tensor_tensor(X[:, half, :], X[:, half, :], YS[:, 0, half, :], ALU.add).then_inc(s_fin, 1)


_INS = ["x", "cond_2048", "L0_cond_Wq", "L0_cond_Wo", "L0_ffn_gate_w", "L0_ffn_w1", "L0_ffn_w2", "L0_ffn_w3",
        "L0_ffn_sw1", "L0_ffn_sw2", "L0_ffn_sw3"]


def constants():
    import numpy as np

    p = np.arange(P)
    c = np.zeros((P, NCONST), np.float32)
    c[:, C_ID:C_ID + P] = np.eye(P)
    c[:, C_UP:C_UP + P] = p[:, None] < p[None, :]
    for k in range(2):
        for part in range(2):
            for h in range(2):
                c[4 * k + 2 * part + h, C_SEL + (2 * k + h) * P:C_SEL + (2 * k + h + 1) * P] = 1
    c[:, C_IOTA:C_IOTA + E] = np.arange(E)
    c[:, C_SPLIT] = -(p // 32 % 2)
    c[:, C_SPLIT + 1] = -(p // 16 % 2)
    c[:, C_TRASH] = TRASH + p
    c[:, C_DIAG:C_DIAG + NB] = p[:, None] % 32 == np.arange(NB)
    i = np.zeros((P, NB + 2), np.int32)
    i[:, :NB] = p[:, None] + P * np.arange(NB)
    i[:, NB:] = TOK + p[:, None] + P * np.arange(2)
    return c, i


def kernel(**inputs):
    import numpy as _np
    import concourse.bacc as _bacc
    from concourse import mybir as _mybir
    from concourse.bass_utils import run_bass_kernel_spmd as _run

    nc = _bacc.Bacc("TRN2", target_bir_lowering=False, num_devices=1)
    arrays, args = {}, []
    given = [_np.ascontiguousarray(inputs[name]) for name in _INS] + list(constants())
    for name, a in zip(_INS + ["constants", "token_numbers"], given):
        arrays[f"in_{name}"] = a
        args.append(nc.dram_tensor(f"in_{name}", a.shape, _mybir.dt.from_np(a.dtype), kind="ExternalInput").ap())
    out = nc.dram_tensor("out_0", (NB, D, T), _mybir.dt.float32, kind="ExternalOutput").ap()
    build(nc, *args, out)
    r = _run(nc, [arrays], core_ids=[0])
    return r.results[0]["out_0"]
```

```python
from contextlib import ExitStack

import concourse.bass as bass
from concourse import mybir

F32 = mybir.dt.float32
F32R = mybir.dt.float32r
I32 = mybir.dt.int32
U32 = mybir.dt.uint32
ALU = mybir.AluOpType
ACT = mybir.ActivationFunctionType
AX = mybir.AxisListType

P = 128
NB, D, T = 8, 128, 256
NH, DK = 8, 16
E, TOPK, CAP = 32, 6, 256
INTER, SI = 176, 352
TOK = NB * D
STEPS = NB * NH // 2
ROW = T + E + 1
TRASH = E * CAP
YROWS = TOK + CAP
DV = DK + 1
HL = 32 + NB
HEADW = 128
TAIL = 64
GAP = HEADW + TAIL - INTER
UPW = 2 * INTER + GAP

C_ID, C_UP = 0, 128
C_SEL = 256
C_IOTA = C_SEL + 4 * P
C_SPLIT = C_IOTA + E
C_TRASH = C_SPLIT + 2
C_DIAG = C_TRASH + 1
NCONST = C_DIAG + NB


def wait_apart(engine, signal, value, met, met_value):
    if not isinstance(value, int):
        register = engine.alloc_register()
        engine.reg_add(register, value, 0)
        value = register
    engine.wait_ge(met, met_value)
    engine.wait_ge(signal, value)


def build(nc, x, cond, wq, wo, gate_w, w1, w2, w3, sw1, sw2, sw3, cst, csti, out):
    ctx = ExitStack()
    with ctx:
        def sb(name, shape, dt=F32):
            return ctx.enter_context(nc.sbuf_tensor(name, shape, dt))

        def sem(name):
            return ctx.enter_context(nc.semaphore(name))

        rows_dram = nc.dram_tensor("expert_rows", [TRASH + P, ROW], F32).ap()
        y_dram = [nc.dram_tensor(f"y{i}", [YROWS, T], F32).ap() for i in range(2)]

        ps = ctx.enter_context(nc.psum_tensor("ps", [P, 8, 512], F32))

        X = sb("X", [P, NB, T])
        SW13 = sb("SW13", [P, 2, 2, SI])
        SW2 = sb("SW2", [P, 3, T])
        RING = 4
        WU = [sb(f"WU_{i}", [P, 2, UPW]) for i in range(RING)]
        W2 = [sb(f"W2_{i}", [P, 2, T]) for i in range(RING)]
        XB = [sb(f"XB{i}", [P, 2, ROW]) for i in range(RING)]
        C = sb("C", [P, NCONST])
        CI = sb("CI", [P, NB + 2], I32)
        IDENT = C[:, C_ID:C_ID + P]
        ZERO = sb("ZERO", [P, T])
        FILL = sb("FILL", [P, 2, ROW])

        s_w = sem("shared_weights_loaded")
        s_ew = [sem(f"expert_weights_loaded{i}") for i in range(RING)]
        s_xb = [sem(f"expert_rows_loaded{i}") for i in range(RING)]
        s_yzero = sem("y_zeroed")

        def load_expert(sp, e, m):
            w3e = w3[e].rearrange("(k p) n -> p k n", p=P)
            sp.dma_start(WU[m][:, :, 0:INTER], w1[e].rearrange("(k p) n -> p k n", p=P)).then_inc(s_ew[m], 16)
            sp.dma_start(WU[m][:, :, INTER + GAP:INTER + TAIL], w3e[:, :, HEADW:INTER]).then_inc(s_ew[m], 16)
            sp.dma_start(WU[m][:, :, INTER + TAIL:UPW], w3e[:, :, 0:HEADW]).then_inc(s_ew[m], 16)
            sp.dma_start(W2[m][0:HEADW, 0, :], w2[e, 0:HEADW, :]).then_inc(s_ew[m], 16)
            sp.dma_start(W2[m][:, 1, :], w2[e, INTER - TAIL:INTER, :].unsqueeze(0).broadcast_to([2, TAIL, T])).then_inc(s_ew[m], 16)

        def load_rows(sp, e, m):
            sp.dma_start(XB[m][:], rows_dram[bass.ds(e * CAP, CAP)].rearrange("(k p) c -> p k c", p=P)).then_inc(s_xb[m], 16)

        attention(nc, sb, sem, ps, x, cond, wq, wo, gate_w, sw1, sw2, sw3, cst, csti,
                  rows_dram, y_dram, X, SW13, SW2, C, CI, IDENT, ZERO, FILL, WU, s_w, s_yzero,
                  load_expert, load_rows)
        experts(nc, sb, sem, ps, y_dram, X, XB, WU, W2, IDENT, s_ew, s_xb, s_yzero,
                load_expert, load_rows, out)


def attention(nc, sb, sem, ps, x, cond, wq, wo, gate_w, sw1, sw2, sw3, cst, csti,
              rows_dram, y_dram, X, SW13, SW2, C, CI, IDENT, ZERO, FILL, WU, s_w, s_yzero,
              load_expert, load_rows):
    with ExitStack() as ctx:
        def sb(name, shape, dt=F32):
            return ctx.enter_context(nc.sbuf_tensor(name, shape, dt))

        MASKB = sb("MASKB", [P, NB, T])
        XM = sb("XM", [P, NB, T])
        XI = sb("XI", [P, NB, T])
        INVC = sb("INVC", [HL, T])
        INVD = sb("INVD", [HL, NB, T], F32R)
        XV = sb("XV", [P, T])
        COND = sb("COND", [HL, T])
        WQ = sb("WQ", [P, D])
        WO = sb("WO", [P, D])
        WOT = sb("WOT", [P, P])
        GW = sb("GW", [E, T])
        GWT = sb("GWT", [P, 2, E])
        MASKT = sb("MASKT", [P, 2, NB])
        WQT = sb("WQT", [P, D])
        WQR = sb("WQR", [P, 4, 2, 4, DK])
        SEL = sb("SEL", [8, 2, 2, P], F32R)
        UP = sb("UP", [P, P], F32R)
        MASKED = sb("MASKED", [NB, 1])
        XS = sb("XS", [P, HL])
        SV = sb("SV", [HL, 2, 4, 32], F32R)
        HI = sb("HI", [P, 2, T], F32R)
        QA = sb("QA", [P, 4, T], F32R)
        QB = sb("QB", [P, 4, T], F32R)
        VS = sb("VS", [P, 2, NH, DV])
        VP = sb("VP", [P, 2, NH, DV])
        EX = sb("EX", [P, 4, 2, 2, T])
        NEGMAX = sb("NEGMAX", [P, 2, 2])
        NM2 = sb("NM2", [P, 2, 2, 2])
        NMT = sb("NMT", [8, P], F32R)
        U = sb("U", [P, 2, T])
        RDEN = sb("RDEN", [P, 2 * NH, 1])
        CTX = sb("CTX", [P, 2, P])
        CTT = sb("CTT", [P, T])
        PAY = sb("PAY", [P, ROW])
        YT = sb("YT", [P, 2, P])
        LG = sb("LG", [P, E])
        TOP = sb("TOP", [P, 8])
        TOPI = sb("TOPI", [P, 8], U32)
        TOPF = sb("TOPF", [P, 8])
        NTOP = sb("NTOP", [P, 1])
        ESUM = sb("ESUM", [P, 1])
        RSUM = sb("RSUM", [P, 1])
        ES = sb("ES", [P, E])
        ONEH = sb("ONEH", [P, TOPK, E])
        PICK = sb("PICK", [P, TOPK, E])
        CHOSEN = sb("CHOSEN", [P, E], F32R)
        BEFORE = sb("BEFORE", [P, E], F32R)
        ONES = sb("ONES", [P, P], F32R)
        PLACE = sb("PLACE", [P, TOPK])
        FITS = sb("FITS", [P, TOPK])
        SLOTF = sb("SLOTF", [P, TOPK])
        SLOT = sb("SLOT", [P, TOPK], I32)

        s_wload = sem("wq_wo_gate_consts_loaded")
        s_first = sem("x_and_mask_of_batch_0_loaded")
        s_x0 = sem("x_loaded")
        s_mask = sem("mask_loaded")
        s_rowfill = sem("rows_filled")
        s_pre = sem("pool_prepared")
        s_tset = sem("setup_transposed")
        s_eset = sem("setup_copied")
        s_wqr = sem("wq_spread")
        s_xm0 = sem("x_of_batch_0_masked")
        s_xm = sem("x_masked")
        s_invc = sem("mask_subtracted")
        s_xi = sem("masked_x_ready")
        s_xs = sem("x_summed")
        s_svp = sem("masked_v_summed")
        s_sv = sem("masked_v_copied")
        s_invd = sem("mask_inverted")
        s_svl = sem("masked_v_split")
        s_cond = sem("condition_loaded")
        s_zero = sem("paddings_zeroed")
        s_gap = sem("expert_gaps_zeroed")
        s_vs = sem("v_staged")
        s_u = sem("pv_copied")
        s_ut = sem("pv_transposed")
        s_pj = sem("q_projected")
        s_vp = sem("v_projected")
        s_hi = sem("high_part_ready")
        s_ab = sem("q_operands_ready")
        s_xv = sem("xv_ready")
        s_ve = sem("v_ready")
        s_sc = sem("scores_ready")
        s_nm = sem("negmax_ready")
        s_nt = sem("negmax_transposed")
        s_nc = sem("negmax_copied")
        s_sh = sem("scores_shifted")
        s_ex = sem("exp_ready")
        s_pv = sem("pv_ready")
        s_ct = sem("context_ready")
        s_ctt = sem("context_transposed")
        s_ctc = sem("context_copied")
        s_wo = sem("out_projected")
        s_y = sem("y_copied")
        s_ytc = sem("yt_copied")
        s_xfh = sem("xf_high_ready")
        s_lg = sem("logits_ready")
        s_top = sem("top_found")
        s_es = sem("router_exp_ready")
        s_ch = sem("choices_ready")
        s_ct2 = sem("choices_counted")
        s_lgc = sem("logits_copied")
        s_place = sem("places_ready")
        s_rs = sem("router_sum_inverted")
        s_slot = sem("slots_ready")
        s_scat = sem("rows_scattered")
        s_dve = sem("vector_in_order")
        s_pool = sem("pool_in_order")

        NG = 3
        GW_ = [min(P, SI - i * P) for i in range(NG)]
        CH = TOK // T
        SGS = [sb(f"SGS{i}", [P, T]) for i in range(2)]
        HS = sb("HS", [P, NG, T])
        XFH = sb("XFH", [P, 2, TOK], F32R)
        XFL = sb("XFL", [P, 2, TOK], F32R)
        SW13H = sb("SW13H", [P, 2, 2, SI], F32R)
        SW13L = sb("SW13L", [P, 2, 2, SI], F32R)
        SW2H = sb("SW2H", [P, NG, T], F32R)
        SW2L = sb("SW2L", [P, NG, T], F32R)
        HSH = sb("HSH", [P, NG, T], F32R)
        HSL = sb("HSL", [P, NG, T], F32R)

        s_swh = sem("shared_weights_high_ready")
        s_swl = sem("shared_weights_low_ready")
        s_hsh = sem("shared_h_high_ready")
        s_hsl = sem("shared_h_low_ready")
        s_xfl = sem("xf_low_ready")
        s_sup = sem("shared_up_ready")
        s_ssg = sem("shared_silu_ready")
        s_hs = sem("shared_h_ready")
        s_sdn = sem("shared_down_ready")
        s_res = sem("residual_ready")

        B_PO, B_PJ, B_NM, B_FIN = 4, 5, 6, 7

        def scores(t2):
            return ps[:, 2 * t2:2 * t2 + 2, :]

        block = ctx.enter_context(nc.Block())

        @block.sync
        def _(sp):
            sp.dma_start(WQ[:], wq).then_inc(s_wload, 16)
            sp.dma_start(C[:], cst).then_inc(s_wload, 16)
            sp.dma_start(X[:, 0, :], x[0]).then_inc(s_first, 16)
            sp.dma_start(MASKB[:, 0, :], cond[0:1, :].broadcast_to([P, T])).then_inc(s_first, 16)
            sp.dma_start(WO[:], wo).then_inc(s_wload, 16)
            sp.dma_start(GW[:], gate_w).then_inc(s_wload, 16)
            sp.wait_ge(s_zero, 1)
            for n in range(2):
                sp.dma_start(COND[32 * n:32 * n + NB, :], cond).then_inc(s_cond, 16)
            sp.dma_start(CI[:], csti).then_inc(s_wload, 16)
            sp.dma_start(X[:, 1:NB, :], x[1:NB].rearrange("b p t -> p b t")).then_inc(s_x0, 16)
            sp.dma_start(MASKB[:, 1:NB, :].rearrange("p b t -> p (b t)"),
                         cond.rearrange("(a b) t -> a (b t)", a=1)[:, T:NB * T].broadcast_to([P, (NB - 1) * T])).then_inc(s_mask, 16)
            sp.wait_ge(s_pre, 1)
            for k in range(2):
                sp.dma_start(rows_dram[0:TRASH].rearrange("(e k p) c -> k p e c", k=2, p=P)[k],
                             FILL[:, k:k + 1, :].broadcast_to([P, E, ROW])).then_inc(s_rowfill, 16)
            for y in y_dram:
                sp.dma_start(y.rearrange("(n p) t -> p n t", p=P),
                             ZERO[:].unsqueeze(1).broadcast_to([P, YROWS // P, T])).then_inc(s_yzero, 16)
            for i, w in enumerate((sw1, sw3)):
                sp.dma_start(SW13[:, :, i, :], w.rearrange("(k p) n -> p k n", p=P)).then_inc(s_w, 16)
            for i in range(3):
                k = min(P, SI - i * P)
                sp.dma_start(SW2[0:k, i, :], sw2[i * P:i * P + k, :]).then_inc(s_w, 16)
            sp.wait_ge(s_gap, 1)
            for e in range(4):
                load_expert(sp, e, e)
            sp.wait_ge(s_scat, 16 * TOPK * NB)
            for e in range(4):
                load_rows(sp, e, e)

        @block.gpsimd
        def _(po):
            nc.gpsimd.memset(COND[:], 0.0).then_inc(s_zero, 1)
            for m in range(len(WU)):
                ins = nc.gpsimd.memset(WU[m][:, :, INTER:INTER + GAP], 0.0)
            ins.then_inc(s_gap, 1)
            order = [0]

            def link(ins):
                order[0] += 1
                ins.then_inc(s_pool, 1)
                po.wait_ge(s_pool, order[0])

            link(nc.gpsimd.memset(ZERO[:], 0.0))
            link(nc.gpsimd.memset(FILL[:], 0.0))
            po.wait_ge(s_wload, 80)
            nc.gpsimd.tensor_copy(FILL[:, :, ROW - 1], CI[:, NB:NB + 2].bitcast(F32)).then_inc(s_pre, 1)
            nc.gpsimd.memset(ONES[:].bitcast(F32), 1.0)
            nc.gpsimd.memset(BEFORE[:].bitcast(F32), 0.0)
            po.wait_ge(s_x0, 16)
            po.wait_ge(s_mask, 16)
            nc.gpsimd.tensor_tensor(XM[:, 1:NB, :], X[:, 1:NB, :], MASKB[:, 1:NB, :], ALU.mult).then_inc(s_xm, 1)
            po.wait_ge(s_xm0, 1)
            po.wait_ge(s_xm, 1)
            nc.gpsimd.tensor_tensor(XI[:], X[:], XM[:], ALU.subtract).then_inc(s_xi, 1)
            po.wait_ge(s_eset, 1)

            def values(b, used):
                po.wait_ge(s_vs, b + 1)
                if used:
                    po.wait_ge(s_pv, 2 * b)
                nc.gpsimd.tensor_copy(VP[:, :, :, DK], MASKT[:, :, bass.ds(b, 1)].broadcast_to([P, 2, NH]))
                nc.gpsimd.tensor_copy(VP[:, :, :, 0:DK].rearrange("p k h d -> p (k h) d"),
                                      VS[:, :, :, 0:DK].rearrange("p k h d -> p (k h) d")).then_inc(s_ve, 1)

            values(0, False)
            po.wait_ge(s_invc, 1)
            nc.gpsimd.tensor_tensor(INVD[:], INVC[:].unsqueeze(1).broadcast_to([HL, NB, T]),
                                    C[0:HL, C_DIAG:C_DIAG + NB].unsqueeze(2).broadcast_to([HL, NB, T]), ALU.mult).then_inc(s_invd, 1)
            po.wait_ge(s_rowfill, 32)

            def low_features(b):
                wait_apart(po, s_xfh, b + 1, s_rowfill, 32)
                nc.gpsimd.tensor_tensor(XFL[:, :, bass.ds(b * P, P)], YT[:], XFH[:, :, bass.ds(b * P, P)].bitcast(F32),
                                        ALU.subtract).then_inc(s_xfl, 1)

            def scatter(b, used):
                if used:
                    po.wait_ge(s_scat, 16 * TOPK * b)
                nc.gpsimd.tensor_copy(PAY[:, ROW - 1:ROW], CI[:, bass.ds(b, 1)].bitcast(F32)).then_inc(s_slot, 1)
                wait_apart(po, s_place, b + 1, s_rowfill, 32)
                nc.gpsimd.tensor_scalar(FITS[:], PLACE[:], float(CAP), None, ALU.is_lt).then_inc(s_slot, 1)
                nc.gpsimd.tensor_scalar(SLOTF[:], TOPF[:, 0:TOPK], float(CAP), C[:, C_TRASH:C_TRASH + 1],
                                        ALU.mult, ALU.subtract).then_inc(s_slot, 1)
                wait_apart(po, s_slot, 7 * b + 3, s_rowfill, 32)
                nc.gpsimd.tensor_tensor(SLOTF[:], SLOTF[:], PLACE[:], ALU.add).then_inc(s_slot, 1)
                wait_apart(po, s_slot, 7 * b + 4, s_rowfill, 32)
                nc.gpsimd.tensor_tensor(SLOTF[:], SLOTF[:], FITS[:], ALU.mult).then_inc(s_slot, 1)
                wait_apart(po, s_slot, 7 * b + 5, s_rowfill, 32)
                nc.gpsimd.tensor_scalar(SLOT[:], SLOTF[:], C[:, C_TRASH:C_TRASH + 1], None, ALU.add).then_inc(s_slot, 1)
                wait_apart(po, s_rs, b + 1, s_rowfill, 32)
                nc.gpsimd.tensor_scalar(PAY[:, T:T + E], ES[:], RSUM[:, 0:1], None, ALU.mult).then_inc(s_slot, 1)
                wait_apart(po, s_slot, 7 * b + 7, s_rowfill, 32)
                for k in range(TOPK):
                    po.indirect_dma_start(out=rows_dram, out_offset=bass.IndirectOffsetOnAxis(ap=SLOT[:, k:k + 1], axis=0),
                                          in_=PAY[:], in_offset=None).then_inc(s_scat, 16)

            values(1, True)
            values(2, True)
            po.wait_ge(s_swh, 3)
            nc.gpsimd.tensor_tensor(SW13L[:], SW13[:], SW13H[:].bitcast(F32), ALU.subtract).then_inc(s_swl, 1)
            nc.gpsimd.tensor_tensor(SW2L[:, 0:2, :], SW2[:, 0:2, :], SW2H[:, 0:2, :].bitcast(F32), ALU.subtract).then_inc(s_swl, 1)
            nc.gpsimd.tensor_tensor(SW2L[0:GW_[2], 2, :], SW2[0:GW_[2], 2, :], SW2H[0:GW_[2], 2, :].bitcast(F32),
                                    ALU.subtract).then_inc(s_swl, 1)
            low_features(0)
            scatter(0, False)
            with po.Fori(3, NB - 1) as b:
                values(b, True)
                low_features(b - 2)
                scatter(b - 2, True)
            values(NB - 1, True)
            low_features(NB - 3)
            scatter(NB - 3, True)
            low_features(NB - 2)
            scatter(NB - 2, True)
            low_features(NB - 1)
            scatter(NB - 1, True)
            po.wait_ge(s_scat, 16 * TOPK * NB)

        @block.tensor
        def _(pe):
            pe.wait_ge(s_wload, 80)
            pe.wait_ge(s_cond, 32)
            nc.tensor.transpose(ps[:, B_PJ, 0:P], WQ[:], IDENT)
            for k in range(2):
                nc.tensor.transpose(ps[:, B_PJ, P + k * E:P + (k + 1) * E], GW[:, k * P:(k + 1) * P], C[0:E, C_ID:C_ID + E])
            for k in range(2):
                nc.tensor.transpose(ps[:, B_PJ, 192 + k * NB:192 + (k + 1) * NB], COND[0:NB, k * P:(k + 1) * P],
                                    C[0:NB, C_ID:C_ID + NB])
            nc.tensor.transpose(ps[:, B_PJ, 256:256 + P], WO[:], IDENT).then_inc(s_tset, 1)

            def project(b, half):
                for i in range(2):
                    ins = nc.tensor.matmul(ps[:, B_PJ, i * T:(i + 1) * T],
                                           WQR[:, 2 * half + i].rearrange("p h r d -> p (h r d)"),
                                           XM[:, bass.ds(b, 1), :].rearrange("p a t -> p (a t)"), start=True, stop=True)
                ins.then_inc(s_pj, 1)

            def project_v(b):
                pe.wait_ge(s_xv, b + 1)
                for k in range(2):
                    ins = nc.tensor.matmul(ps[:, B_PJ, k * P:(k + 1) * P], XV[:, k * P:(k + 1) * P], WQT[:],
                                           start=True, stop=True)
                ins.then_inc(s_vp, 1)

            def score(b, j, free):
                if free:
                    pe.wait_ge(s_ex, 4 * b + j - 1)
                if j in (0, 2):
                    pe.wait_ge(s_ab, 2 * b + 1 + j // 2)
                for hh in range(2):
                    for k in range(2):
                        ins = nc.tensor.matmul(scores(j % 2)[:, hh, k * T:(k + 1) * T],
                                               QA[64 * hh:64 * hh + 64, j, k * P:(k + 1) * P],
                                               QB[64 * hh:64 * hh + 64, j, :], start=(k == 0), stop=False,
                                               skip_group_check=True)
                ins.then_inc(s_sc, 1)

            def shift(b, j):
                pe.wait_ge(s_nc, 4 * b + j + 1)
                for hh in range(2):
                    for q in range(2):
                        ins = nc.tensor.matmul(
                            scores(j % 2)[:, hh, :].rearrange("p (k t) -> p k t", k=2)[:, :, q * P:(q + 1) * P], SEL[:, q, hh, :],
                            NMT[:].unsqueeze(1).broadcast_to([8, 2, P]), start=False, stop=True, skip_group_check=True)
                ins.then_inc(s_sh, 1)

            def weigh(b, g, po_used):
                pe.wait_ge(s_ex, 4 * b + 2 * g + 2)
                if g == 0:
                    pe.wait_ge(s_ve, b + 1)
                    if po_used:
                        pe.wait_ge(s_u, b)
                    for n in range(2):
                        nc.tensor.matmul(ps[:, B_PO, n * T:(n + 1) * T], SV[:, n].rearrange("p i d -> p (i d)"),
                                         INVD[:, bass.ds(b, 1), :].rearrange("p a n -> p (a n)"),
                                         start=(n == 0), stop=False, skip_group_check=True)
                for k in range(2):
                    for i in range(4):
                        h = 4 * g + i
                        ins = nc.tensor.matmul(ps[32 * i:32 * i + DV, B_PO, g * T:(g + 1) * T], VP[:, k, h, :],
                                               EX[:, h // 2, h % 2, k, :], start=False, stop=(k == 1),
                                               skip_group_check=True)
                ins.then_inc(s_pv, 1)

            def turn_max(b, j):
                pe.wait_ge(s_nm, 4 * b + j + 1)
                nc.tensor.transpose(ps[0:8, B_NM, 0:P], NM2[:].rearrange("p k r h -> p (k r h)"), IDENT).then_inc(s_nt, 1)

            def turn_sums(b, used):
                if used:
                    pe.wait_ge(s_place, b)
                pe.wait_ge(s_u, b + 1)
                for q in range(2):
                    for g in range(2):
                        ins = nc.tensor.transpose(ps[:, B_FIN, (2 * q + g) * P:(2 * q + g + 1) * P], U[:, g, q * P:(q + 1) * P], IDENT)
                ins.then_inc(s_ut, 1)

            def turn_context(b):
                pe.wait_ge(s_ct, b + 1)
                for q in range(2):
                    ins = nc.tensor.transpose(ps[:, B_FIN, q * P:(q + 1) * P], CTX[:, q, :], IDENT)
                ins.then_inc(s_ctt, 1)

            def out_project(b):
                pe.wait_ge(s_ctc, b + 1)
                for k in range(2):
                    ins = nc.tensor.matmul(ps[:, B_FIN, T + k * P:T + (k + 1) * P], CTT[:, k * P:(k + 1) * P], WOT[:],
                                           start=True, stop=True)
                ins.then_inc(s_wo, 1)

            def logits(b):
                pe.wait_ge(s_xfh, b + 1)
                for k in range(2):
                    ins = nc.tensor.transpose(ps[:, B_FIN, E + k * P:E + (k + 1) * P], YT[:, k, :], IDENT)
                for k in range(2):
                    ins = nc.tensor.matmul(ps[:, B_FIN, 0:E], YT[:, k, :], GWT[:, k, :], start=(k == 0), stop=(k == 1))
                ins.then_inc(s_lg, 1)

            def count(b):
                pe.wait_ge(s_ch, b + 1)
                pe.wait_ge(s_y, b + 1)
                nc.tensor.matmul(ps[:, B_FIN, 0:E], UP[:], CHOSEN[:], start=True, stop=False)
                nc.tensor.matmul(ps[:, B_FIN, 0:E], ONES[:], BEFORE[:], start=False, stop=True).then_inc(s_ct2, 1)

            def step(b, j, has_prev, has_prev2, has_next, first=False):
                if j < 3:
                    score(b, j + 1, has_prev or j > 0)
                elif has_next:
                    score(b + 1, 0, True)
                shift(b, j)
                if j == 0 and has_prev2:
                    logits(b - 2)
                if j == 3 and has_prev:
                    turn_context(b - 1)
                if not has_prev and j == 1:
                    pe.wait_ge(s_xs, 1)
                    nc.tensor.matmul(ps[0:HL, B_FIN, 0:P], XS[:], WQT[:], start=True, stop=True).then_inc(s_svp, 1)
                if not has_prev and j == 2:
                    pe.wait_ge(s_svl, 1)
                    pe.wait_ge(s_invd, 1)
                if j == 2:
                    weigh(b, 0, has_prev)
                if j == 0 and has_prev:
                    weigh(b - 1, 1, True)
                if j == 1:
                    if has_next:
                        pe.wait_ge(s_vs, b + 2)
                        project(b + 1, 0)
                    if has_prev2:
                        count(b - 2)
                if j == 3 and has_next:
                    pe.wait_ge(s_ab, 2 * b + 3)
                    project(b + 1, 1)
                if j < 3:
                    turn_max(b, j + 1)
                elif has_next:
                    turn_max(b + 1, 0)
                if j == 0 and has_next:
                    pe.wait_ge(s_ab, 2 * b + 2)
                    project_v(b + 1)
                if j == 2 and has_prev:
                    turn_sums(b - 1, has_prev2)
                if j == 3 and has_prev:
                    out_project(b - 1)

            pe.wait_ge(s_wqr, 3)
            pe.wait_ge(s_xm0, 1)
            project(0, 0)
            pe.wait_ge(s_ab, 1)
            project(0, 1)
            pe.wait_ge(s_eset, 2)
            score(0, 0, False)
            turn_max(0, 0)
            pe.wait_ge(s_ab, 2)
            project_v(0)
            for j in range(4):
                step(0, j, False, False, True, first=True)
            for j in range(4):
                step(1, j, True, False, True)
            for j in range(4):
                step(2, j, True, True, True, first=True)
            with pe.Fori(3, NB - 1) as b:
                for j in range(4):
                    step(b, j, True, True, True)
            for j in range(4):
                step(NB - 1, j, True, True, False)

            def shared_up(c, i):
                if NG * c + i >= 2:
                    pe.wait_ge(s_hs, NG * c + i - 1)
                for u in range(2):
                    for n, (k, w, xf) in enumerate((k, w, xf) for k in range(2) for w, xf in ((SW13H, XFH), (SW13H, XFL), (SW13L, XFH))):
                        ins = nc.tensor.matmul(ps[0:GW_[i], 2 * ((NG * c + i) % 2) + u, 0:T], w[:, k, u, i * P:i * P + GW_[i]],
                                               xf[:, k, c * T:(c + 1) * T], start=(n == 0), stop=(n == 5))
                ins.then_inc(s_sup, 1)

            def shared_down(c):
                if c:
                    pe.wait_ge(s_res, c)
                for i in range(NG):
                    pe.wait_ge(s_hsl, NG * c + i + 1)
                    for st in range(2):
                        for n, (h, w) in enumerate(((HSH, SW2H), (HSH, SW2L), (HSL, SW2H))):
                            ins = nc.tensor.matmul(ps[:, B_PJ, st * T:(st + 1) * T], h[0:GW_[i], i, st * P:(st + 1) * P],
                                                   w[0:GW_[i], i, :], start=(i == 0 and st == 0 and n == 0),
                                                   stop=(i == NG - 1 and n == 2), skip_group_check=True)
                ins.then_inc(s_sdn, 1)

            weigh(NB - 1, 1, True)
            logits(NB - 2)
            pe.wait_ge(s_swl, 3)
            pe.wait_ge(s_xfl, 2)
            shared_up(0, 0)
            shared_up(0, 1)
            count(NB - 2)
            shared_up(0, 2)
            turn_sums(NB - 1, True)
            pe.wait_ge(s_xfl, 4)
            shared_up(1, 0)
            shared_down(0)
            turn_context(NB - 1)
            shared_up(1, 1)
            out_project(NB - 1)
            shared_up(1, 2)
            logits(NB - 1)
            pe.wait_ge(s_xfl, 6)
            shared_up(2, 0)
            shared_down(1)
            count(NB - 1)
            shared_up(2, 1)
            shared_up(2, 2)
            pe.wait_ge(s_xfl, NB)
            shared_up(3, 0)
            shared_down(2)
            shared_up(3, 1)
            shared_up(3, 2)
            shared_down(3)

        @block.scalar
        def _(act):
            act.wait_ge(s_tset, 1)
            nc.scalar.activation(WQT[:], ps[:, B_PJ, 0:P], ACT.Copy).then_inc(s_wqr, 1)
            nc.scalar.activation(MASKT[:].rearrange("p k b -> p (k b)"), ps[:, B_PJ, 192:192 + 2 * NB], ACT.Copy).then_inc(s_eset, 1)
            nc.scalar.activation(GWT[:].rearrange("p k b -> p (k b)"), ps[:, B_PJ, P:P + 2 * E], ACT.Copy)
            nc.scalar.activation(WOT[:], ps[:, B_PJ, 256:256 + P], ACT.Copy).then_inc(s_wqr, 1)
            nc.scalar.activation(UP[:], C[:, C_UP:C_UP + P], ACT.Copy)
            nc.scalar.activation(SEL[:].rearrange("p q h n -> p (q h n)"), C[0:8, C_SEL:C_SEL + 4 * P], ACT.Copy).then_inc(s_eset, 1)

            def high(b, half, first=False):
                act.wait_ge(s_pj, 2 * b + 1 + half)
                if not first:
                    act.wait_ge(s_ab, 2 * b + half)
                nc.scalar.activation(HI[:].rearrange("p i t -> p (i t)"), ps[:, B_PJ, :], ACT.Copy).then_inc(s_hi, 1)

            def negmax(b, j):
                act.wait_ge(s_nt, 4 * b + j + 1)
                nc.scalar.activation(NMT[:], ps[0:8, B_NM, 0:P], ACT.Copy).then_inc(s_nc, 1)

            def exps(b, j, used):
                act.wait_ge(s_sh, 4 * b + j + 1)
                if used:
                    act.wait_ge(s_pv, 2 * b - 1 + j // 2)
                nc.scalar.activation(EX[:, j].rearrange("p h k t -> p h (k t)"), scores(j % 2), ACT.Exp,
                                     scale=float(DK) ** -0.5).then_inc(s_ex, 1)

            def turned_x(b):
                act.wait_ge(s_vp, b)
                nc.scalar.activation(XV[:], XM[:, bass.ds(b, 1), :].rearrange("p a t -> p (a t)"), ACT.Copy).then_inc(s_xv, 1)

            def masked_sums():
                act.wait_ge(s_svp, 1)
                nc.scalar.activation(SV[:, :, :, 0:DK].rearrange("p g i d -> p (g i) d"),
                                     ps[0:HL, B_FIN, 0:P].rearrange("p (h d) -> p h d", h=NH), ACT.Copy).then_inc(s_sv, 1)

            def values(b, used=True):
                act.wait_ge(s_vp, b + 1)
                if used:
                    act.wait_ge(s_ve, b)
                nc.scalar.activation(VS[:, :, :, 0:DK].rearrange("p k h d -> p (k h) d"),
                                     ps[:, B_PJ, 0:2 * P].rearrange("p (k h d) -> p (k h) d", k=2, h=NH),
                                     ACT.Copy).then_inc(s_vs, 1)

            def keep_sums(b, used):
                act.wait_ge(s_pv, 2 * b + 2)
                if used:
                    act.wait_ge(s_ut, b)
                nc.scalar.activation(U[:].rearrange("p g t -> p (g t)"), ps[:, B_PO, :], ACT.Copy).then_inc(s_u, 1)

            def keep_context(b):
                act.wait_ge(s_ctt, b + 1)
                nc.scalar.activation(CTT[:], ps[:, B_FIN, 0:T], ACT.Copy).then_inc(s_ctc, 1)

            def keep_y(b, used):
                act.wait_ge(s_wo, b + 1)
                if used:
                    act.wait_ge(s_xfl, b)
                nc.scalar.activation(YT[:].rearrange("p k n -> p (k n)"), ps[:, B_FIN, T:2 * T], ACT.Copy).then_inc(s_ytc, 1)
                nc.scalar.activation(XFH[:, :, bass.ds(b * P, P)], ps[:, B_FIN, T:2 * T].rearrange("p (k n) -> p k n", k=2),
                                     ACT.Copy).then_inc(s_xfh, 1)

            def keep_logits(b, used):
                act.wait_ge(s_lg, b + 1)
                if used:
                    act.wait_ge(s_ch, b)
                nc.scalar.activation(LG[:], ps[:, B_FIN, 0:E], ACT.Copy).then_inc(s_lgc, 1)

            def keep_rows(b, used):
                if used:
                    act.wait_ge(s_scat, 16 * TOPK * b)
                nc.scalar.activation(PAY[:, 0:T], ps[:, B_FIN, E:E + T], ACT.Copy).then_inc(s_y, 1)

            def router_exp(b, used):
                act.wait_ge(s_top, b + 1)
                if used:
                    act.wait_ge(s_slot, 7 * b)
                nc.scalar.activation(ES[:], LG[:], ACT.Exp, bias=NTOP[:], accum_out=ESUM[:]).then_inc(s_es, 1)

            def step(b, j, has_prev, has_prev2, has_next, first=False):
                if j == 1 and has_next:
                    values(b + 1)
                if j == 1 and has_prev2:
                    keep_rows(b - 2, not first)
                if j == 3 and has_prev:
                    keep_context(b - 1)
                exps(b, j, has_prev)
                if j == 0 and has_next:
                    turned_x(b + 1)
                if j == 0 and has_prev:
                    keep_sums(b - 1, has_prev2)
                if j == 0 and has_prev2:
                    keep_logits(b - 2, not first)
                if j == 1 and has_next:
                    high(b + 1, 0)
                if j == 3 and has_next:
                    high(b + 1, 1)
                if j < 3:
                    negmax(b, j + 1)
                elif has_next:
                    negmax(b + 1, 0)
                if j == 0 and has_prev2:
                    router_exp(b - 2, not first)
                if j == 3 and has_prev:
                    keep_y(b - 1, has_prev2)
                if j == 1 and not has_prev:
                    masked_sums()

            high(0, 0, True)
            high(0, 1)
            negmax(0, 0)
            values(0, False)
            act.wait_ge(s_xm, 1)
            for j in range(4):
                step(0, j, False, False, True, first=True)
            for j in range(4):
                step(1, j, True, False, True)
            act.wait_ge(s_w, 80)
            nc.scalar.activation(SW13H[:], SW13[:], ACT.Copy).then_inc(s_swh, 1)
            nc.scalar.activation(SW2H[:, 0:2, :], SW2[:, 0:2, :], ACT.Copy).then_inc(s_swh, 1)
            nc.scalar.activation(SW2H[0:GW_[2], 2, :], SW2[0:GW_[2], 2, :], ACT.Copy).then_inc(s_swh, 1)
            for j in range(4):
                step(2, j, True, True, True, first=True)
            with act.Fori(3, NB - 1) as b:
                for j in range(4):
                    step(b, j, True, True, True)
            for j in range(4):
                step(NB - 1, j, True, True, False)

            def shared_high(c, i):
                t = NG * c + i
                act.wait_ge(s_hs, t + 1)
                if c and i == 0:
                    act.wait_ge(s_sdn, c)
                nc.scalar.activation(HSH[0:GW_[i], i, :], HS[0:GW_[i], i, :], ACT.Copy).then_inc(s_hsh, 1)

            def shared_silu(c, i):
                t = NG * c + i
                act.wait_ge(s_sup, t + 1)
                if t >= 2:
                    act.wait_ge(s_hs, t - 1)
                nc.scalar.activation(SGS[t % 2][0:GW_[i], :], ps[0:GW_[i], 2 * (t % 2), 0:T], ACT.Silu).then_inc(s_ssg, 1)

            keep_sums(NB - 1, True)
            keep_logits(NB - 2, True)
            router_exp(NB - 2, True)
            keep_rows(NB - 2, True)
            shared_silu(0, 0)
            shared_silu(0, 1)
            shared_high(0, 0)
            shared_silu(0, 2)
            shared_high(0, 1)
            shared_high(0, 2)
            shared_silu(1, 0)
            keep_context(NB - 1)
            shared_high(1, 0)
            shared_silu(1, 1)
            keep_y(NB - 1, True)
            shared_high(1, 1)
            shared_silu(1, 2)
            shared_high(1, 2)
            keep_logits(NB - 1, True)
            router_exp(NB - 1, True)
            keep_rows(NB - 1, True)
            for c in (2, 3):
                shared_silu(c, 0)
                for i in range(1, NG):
                    shared_silu(c, i)
                    shared_high(c, i - 1)
                shared_high(c, NG - 1)

        @block.vector
        def _(dve):
            state = {"base": 0, "k": 0}

            def link(ins, apart=False):
                state["k"] += 1
                ins.then_inc(s_dve, 1)
                if apart:
                    wait_apart(dve, s_dve, state["base"] + state["k"], s_mask, 16)
                else:
                    dve.wait_ge(s_dve, state["base"] + state["k"])

            dve.wait_ge(s_first, 32)
            nc.vector.tensor_tensor(XM[:, 0, :], X[:, 0, :], MASKB[:, 0, :], ALU.mult).then_inc(s_xm0, 1)
            dve.wait_ge(s_xm0, 1)
            nc.vector.tensor_copy(XV[:], XM[:, 0, :]).then_inc(s_xv, 1)
            dve.wait_ge(s_wqr, 1)
            nc.vector.tensor_copy(WQR[:].rearrange("p j h r d -> p (j h) r d"),
                                  WQT[:].rearrange("p (h d) -> p h d", h=NH).unsqueeze(2).broadcast_to([P, NH, 4, DK])
                                  ).then_inc(s_wqr, 1)

            def operands(b, half, used, which=(0, 1)):
                dve.wait_ge(s_hi, 2 * b + 1 + half)
                if used:
                    dve.wait_ge(s_sc, 4 * b - 2 + 2 * half)
                q = ps[:, B_PJ, :].rearrange("p (i t) -> p i t", i=2)
                for n in which:
                    dst = (QA, QB)[n]
                    ins = nc.vector.scalar_tensor_tensor(
                        out=dst[:, 2 * half:2 * half + 2, :], in0=HI[:].bitcast(F32),
                        scalar=C[:, C_SPLIT + n:C_SPLIT + n + 1], in1=q, op0=ALU.mult, op1=ALU.add)
                if 1 in which:
                    ins.then_inc(s_ab, 1)

            def negmax(b, j, used):
                dve.wait_ge(s_sc, 4 * b + j + 1)
                link(nc.vector.tensor_reduce(NEGMAX[:], scores(j % 2).rearrange("p h (k t) -> p h k t", k=2),
                                             AX.X, ALU.max, negate=True))
                nm = NEGMAX[:].rearrange("p h k -> p k h")
                if used:
                    dve.wait_ge(s_nt, 4 * b + j)
                link(nc.vector.tensor_copy(NM2[:, :, 0, :].bitcast(F32R), nm))
                nc.vector.tensor_tensor(NM2[:, :, 1, :], nm, NM2[:, :, 0, :], ALU.subtract).then_inc(s_nm, 1)

            def context(b, used):
                dve.wait_ge(s_ut, b + 1)
                sums = ps[:, B_FIN, :].rearrange("p (n d) -> p n d", d=32)
                link(nc.vector.reciprocal(RDEN[:], sums[:, :, DK:DV]))
                if used:
                    dve.wait_ge(s_ctt, b)
                nc.vector.tensor_tensor(CTX[:].rearrange("p q (h d) -> p (q h) d", d=DK), sums[:, :, 0:DK],
                                        RDEN[:].broadcast_to([P, 2 * NH, DK]), ALU.mult).then_inc(s_ct, 1)

            def choose(b, used):
                if used:
                    wait_apart(dve, s_slot, 7 * b, s_mask, 16)
                wait_apart(dve, s_lgc, b + 1, s_mask, 16)
                link(nc.vector.max(TOP[:], LG[:]))
                nc.vector.tensor_scalar(NTOP[:], TOP[:, 0:1], -1.0, None, ALU.mult).then_inc(s_top, 1)
                link(nc.vector.max_index(TOPI[:], TOP[:], LG[:]))
                link(nc.vector.tensor_copy(TOPF[:], TOPI[:]))
                link(nc.vector.tensor_tensor(ONEH[:], C[:, C_IOTA:C_IOTA + E].unsqueeze(1).broadcast_to([P, TOPK, E]),
                                             TOPF[:, 0:TOPK].unsqueeze(2).broadcast_to([P, TOPK, E]), ALU.is_equal))
                with nc.allow_low_precision(reason="zeros and ones"):
                    nc.vector.tensor_reduce(CHOSEN[:], ONEH[:].rearrange("p k e -> p e k"), AX.X, ALU.add).then_inc(s_ch, 1)

            def place(b):
                dve.wait_ge(s_ct2, b + 1)
                link(nc.vector.tensor_tensor(PICK[:], ONEH[:], ps[:, B_FIN, 0:E].unsqueeze(1).broadcast_to([P, TOPK, E]),
                                             ALU.mult))
                nc.vector.tensor_tensor(BEFORE[:], BEFORE[:].bitcast(F32), CHOSEN[:].bitcast(F32), ALU.add)
                nc.vector.tensor_reduce(PLACE[:], PICK[:], AX.X, ALU.add).then_inc(s_place, 1)
                dve.wait_ge(s_es, b + 1)
                nc.vector.reciprocal(RSUM[:], ESUM[:]).then_inc(s_rs, 1)

            def x_sums():
                dve.wait_ge(s_xi, 1)
                link(nc.vector.tensor_reduce(XS[:, 0:NB], XI[:], AX.X, ALU.add))
                nc.vector.tensor_copy(XS[:, 32:HL], XS[:, 0:NB]).then_inc(s_xs, 1)

            def low_sums():
                dve.wait_ge(s_sv, 1)
                low = SV[32:HL, :, :, 0:DK].rearrange("p g i d -> p (g i) d")
                nc.vector.tensor_tensor(low, ps[32:HL, B_FIN, 0:P].rearrange("p (h d) -> p h d", h=NH), low.bitcast(F32),
                                        ALU.subtract).then_inc(s_svl, 1)

            def step(b, j, has_prev, has_prev2, has_next, first=False):
                if j < 3:
                    negmax(b, j + 1, True)
                elif has_next:
                    negmax(b + 1, 0, True)
                if j == 0 and not has_prev:
                    x_sums()
                if j == 1 and not has_prev:
                    low_sums()
                if j == 0 and has_prev2:
                    choose(b - 2, not first)
                if j == 1 and has_prev2:
                    place(b - 2)
                if j == 1 and has_next:
                    operands(b + 1, 0, True, which=(0,))
                if j == 2 and has_next:
                    operands(b + 1, 0, True, which=(1,))
                if j == 2 and has_prev:
                    context(b - 1, has_prev2)
                if j == 3 and has_next:
                    operands(b + 1, 1, True)

            dve.wait_ge(s_cond, 32)
            link(nc.vector.tensor_scalar(INVC[:], COND[:], -1.0, 1.0, ALU.mult, ALU.add))
            link(nc.vector.memset(SV[:].bitcast(F32), 0.0))
            link(nc.vector.memset(XS[:], 0.0))
            link(nc.vector.tensor_reduce(MASKED[:], INVC[0:NB, :], AX.X, ALU.add))
            nc.vector.tensor_copy(SV[0:NB, :, :, DK:DV].rearrange("p g i d -> p (g i) d"),
                                  MASKED[:].unsqueeze(1).broadcast_to([NB, NH, 1])).then_inc(s_invc, 1)
            operands(0, 0, False)
            operands(0, 1, False)
            negmax(0, 0, False)
            for j in range(4):
                step(0, j, False, False, True, first=True)
            for j in range(4):
                step(1, j, True, False, True)
            for j in range(4):
                step(2, j, True, True, True, first=True)
            base, per = state["k"], PER_BATCH
            with dve.Fori(3, NB - 1) as b:
                state["base"], state["k"] = base + (b - 3) * per, 0
                for j in range(4):
                    step(b, j, True, True, True)
                assert state["k"] == per, state["k"]
            state["base"], state["k"] = base + (NB - 4) * per, 0
            for j in range(4):
                step(NB - 1, j, True, True, False)

            def shared_low(c, i):
                dve.wait_ge(s_hsh, NG * c + i + 1)
                nc.vector.tensor_tensor(HSL[0:GW_[i], i, :], HS[0:GW_[i], i, :], HSH[0:GW_[i], i, :].bitcast(F32),
                                        ALU.subtract).then_inc(s_hsl, 1)

            def shared_hidden(c, i):
                t = NG * c + i
                dve.wait_ge(s_ssg, t + 1)
                nc.vector.tensor_tensor(HS[0:GW_[i], i, :], SGS[t % 2][0:GW_[i], :], ps[0:GW_[i], 2 * (t % 2) + 1, 0:T],
                                        ALU.mult).then_inc(s_hs, 1)

            def shared_add(c):
                dve.wait_ge(s_sdn, c + 1)
                xc = X[:, 2 * c:2 * c + 2, :]
                nc.vector.tensor_tensor(xc, xc, ps[:, B_PJ, :].rearrange("p (s t) -> p s t", s=2), ALU.add).then_inc(s_res, 1)

            choose(NB - 2, True)
            shared_hidden(0, 0)
            shared_hidden(0, 1)
            shared_low(0, 0)
            place(NB - 2)
            shared_hidden(0, 2)
            shared_low(0, 1)
            context(NB - 1, True)
            shared_low(0, 2)
            shared_hidden(1, 0)
            shared_add(0)
            shared_low(1, 0)
            shared_hidden(1, 1)
            shared_low(1, 1)
            shared_hidden(1, 2)
            shared_low(1, 2)
            choose(NB - 1, True)
            place(NB - 1)
            shared_hidden(2, 0)
            shared_low(2, 0)
            shared_add(1)
            shared_hidden(2, 1)
            shared_low(2, 1)
            shared_hidden(2, 2)
            shared_low(2, 2)
            shared_hidden(3, 0)
            shared_add(2)
            for i in range(1, NG):
                shared_hidden(3, i)
                shared_low(3, i - 1)
            shared_low(3, NG - 1)
            shared_add(3)


PER_BATCH = 14


def experts(nc, sb, sem, ps, y_dram, X, XB, WU, W2, IDENT, s_ew, s_xb, s_yzero, load_expert, load_rows, out):
    POOLW = INTER + TAIL
    with ExitStack() as ctx:
        def sb(name, shape, dt=F32):
            return ctx.enter_context(nc.sbuf_tensor(name, shape, dt))

        RING = len(WU)
        META = [sb(f"META{i}", [P, 2, 2]) for i in range(RING)]
        META0 = [sb(f"META0_{i}", [P, 2, 2]) for i in range(RING)]
        O = [sb(f"O{i}", [P, 2, T]) for i in range(RING)]
        XTH = [sb(f"XTH{i}", [P, 2, CAP], F32R) for i in range(2)]
        XTL = [sb(f"XTL{i}", [P, 2, CAP], F32R) for i in range(2)]
        WUH = [sb(f"WUH{i}", [P, 2, UPW], F32R) for i in range(2)]
        WUL = [sb(f"WUL{i}", [P, 2, UPW], F32R) for i in range(2)]
        W2H = [sb(f"W2H{i}", [P, 2, T], F32R) for i in range(2)]
        W2L = [sb(f"W2L{i}", [P, 2, T], F32R) for i in range(2)]
        SG = [sb(f"SG{i}", [P, 2, CAP]) for i in range(2)]
        HA = [sb(f"HA{i}", [HEADW, CAP]) for i in range(2)]
        HAH = [sb(f"HAH{i}", [HEADW, CAP], F32R) for i in range(2)]
        HAL = [sb(f"HAL{i}", [HEADW, CAP], F32R) for i in range(2)]
        HB = [sb(f"HB{i}", [TAIL, CAP]) for i in range(2)]
        HBS = [sb(f"HBS{i}", [P, CAP], F32R) for i in range(2)]
        YS = sb("YS", [P, 2, NB, T])

        s_tr = sem("rows_transposed")
        s_xh = sem("xt_high_ready")
        s_xl = sem("xt_low_ready")
        s_wh = sem("up_weights_high_ready")
        s_wlp = sem("up_weights_low_ready_pool")
        s_wld = sem("up_weights_low_ready_vector")
        s_w2h = sem("down_weights_high_ready")
        s_w2l = sem("down_weights_low_ready")
        s_meta0 = sem("meta_read")
        s_meta = sem("meta_ready")
        s_up = sem("up_ready")
        s_sg = sem("silu_ready")
        s_h = sem("h_ready")
        s_hh = sem("h_high_ready")
        s_hl = sem("h_low_ready")
        s_dn = sem("down_ready")
        s_o = sem("weighted_ready")
        s_acc = [sem(f"results_added{i}") for i in range(2)]
        PARTS = 4
        PB = NB // PARTS
        s_yeven = sem("even_sums_loaded")
        s_yodd = [sem(f"odd_sums_loaded{n}") for n in range(PARTS)]
        s_even = sem("even_sums_added")
        s_even_rest = sem("even_sums_added_by_pool")
        s_fin = sem("final_ready")
        s_out = sem("stored")

        B_UP, B_T, B_DN = 0, 4, 6

        def late(e, n):
            return not isinstance(e, int) or e >= n

        def loads(e, m, per):
            return per * (e // 4) + per if isinstance(e, int) else (e - m) * (per // 4) + per

        def pipeline(engine, step):
            for x in range(8):
                step(x, x % 4)
            with engine.Fori(1, (E - 4) // 4) as i:
                for m in range(4):
                    step(4 * i + m + 4, m)
            for x in range(E, E + 4):
                step(x, x % 4)

        def at(part, x, m, behind):
            e = x - behind
            if not isinstance(x, int) or 0 <= e < E:
                part(e, (m - behind) % 4)

        block = ctx.enter_context(nc.Block())

        @block.sync
        def _(sp):
            with sp.Fori(0, (E - 4) // 4) as i:
                for m in range(4):
                    sp.wait_ge(s_meta0, 4 * i + m + 1)
                    sp.wait_ge(s_tr, 4 * i + m + 1)
                    load_rows(sp, 4 * i + m + 4, m)
                    sp.wait_ge(s_wlp, 4 * i + m + 1)
                    sp.wait_ge(s_wld, 4 * i + m + 1)
                    sp.wait_ge(s_w2l, 4 * i + m + 1)
                    load_expert(sp, 4 * i + m + 4, m)
            sp.wait_ge(s_acc[0], 16 * E)
            sp.dma_start(YS[:, 0], y_dram[0][0:TOK].rearrange("(b p) t -> p b t", p=P)).then_inc(s_yeven, 16)
            sp.wait_ge(s_acc[1], 16 * E)
            for n in range(PARTS):
                sp.dma_start(YS[:, 1, n * PB:(n + 1) * PB, :],
                             y_dram[1][n * PB * P:(n + 1) * PB * P].rearrange("(b p) t -> p b t", p=P)).then_inc(s_yodd[n], 16)

        @block.gpsimd
        def _(po):
            po.wait_ge(s_yzero, 32)

            def add(e, m):
                if late(e, 2):
                    wait_apart(po, s_acc[m % 2], (16 * (e - m) if late(e, 4) else 0) + 32 * (m // 2), s_yzero, 32)
                wait_apart(po, s_o, e + 1, s_yzero, 32)
                for k in range(2):
                    po.indirect_dma_start(out=y_dram[m % 2], out_offset=bass.IndirectOffsetOnAxis(
                        ap=META[m][:, k, 1:2].bitcast(I32), axis=0), in_=O[m][:, k, :], in_offset=None,
                        compute_op=ALU.add).then_inc(s_acc[m % 2], 16)

            def low_weights(e, m):
                wait_apart(po, s_wh, e + 1, s_yzero, 32)
                nc.gpsimd.tensor_tensor(WUL[m % 2][:, :, 0:POOLW], WU[m][:, :, 0:POOLW], WUH[m % 2][:, :, 0:POOLW].bitcast(F32),
                                        ALU.subtract).then_inc(s_wlp, 1)

            def step(x, m):
                at(low_weights, x, m, 0)
                at(add, x, m, 4)

            pipeline(po, step)
            for n in range(PARTS // 2, PARTS):
                part = slice(n * PB, (n + 1) * PB)
                wait_apart(po, s_yeven, 16, s_yzero, 32)
                nc.gpsimd.tensor_tensor(X[:, part, :], X[:, part, :], YS[:, 0, part, :], ALU.add).then_inc(s_even_rest, 1)
            for par in range(2):
                po.wait_ge(s_acc[par], 16 * E)

        @block.tensor
        def _(pe):
            def turn(e, m):
                pe.wait_ge(s_xb[m], loads(e, m, 16))
                if late(e, 2):
                    pe.wait_ge(s_xl, e - 1)
                for st in range(2):
                    for k in range(2):
                        ins = nc.tensor.transpose(ps[:, B_T + m % 2, k * CAP + st * P:k * CAP + (st + 1) * P],
                                                  XB[m][:, st, k * P:(k + 1) * P], IDENT)
                ins.then_inc(s_tr, 1)

            def up(e, m):
                n = m % 2
                pe.wait_ge(s_xl, e + 1)
                pe.wait_ge(s_wlp, e + 1)
                pe.wait_ge(s_wld, e + 1)
                if late(e, 2):
                    pe.wait_ge(s_h, e - 1)
                b0 = B_UP + 2 * n
                for a, b, dst in ((0, P, ps[:, b0, 0:CAP]), (INTER - TAIL, INTER + TAIL, ps[:, b0, CAP:2 * CAP]),
                                  (INTER + TAIL, UPW, ps[0:HEADW, b0 + 1, 0:CAP])):
                    for k in range(2):
                        for w, xt in ((WUH, XTH), (WUH, XTL), (WUL, XTH)):
                            ins = nc.tensor.matmul(dst, w[n][:, k, a:b], xt[n][:, k, :],
                                                   start=(k == 0 and w is WUH and xt is XTH), stop=(k == 1 and w is WUL))
                ins.then_inc(s_up, 1)

            def down(e, m):
                n = m % 2
                pe.wait_ge(s_hl, e + 1)
                pe.wait_ge(s_w2l, e + 1)
                if late(e, 2):
                    pe.wait_ge(s_o, e - 1)
                for st in range(2):
                    cols = slice(st * P, (st + 1) * P)
                    dst = ps[:, B_DN + n, st * T:(st + 1) * T]
                    nc.tensor.matmul(dst, HAH[n][:, cols], W2H[n][0:HEADW, 0, :], start=True, stop=False)
                    nc.tensor.matmul(dst, HAH[n][:, cols], W2L[n][0:HEADW, 0, :], start=False, stop=False)
                    nc.tensor.matmul(dst, HAL[n][:, cols], W2H[n][0:HEADW, 0, :], start=False, stop=False)
                    nc.tensor.matmul(dst, HBS[n][:, cols], W2H[n][:, 1, :], start=False, stop=False)
                    ins = nc.tensor.matmul(dst, HBS[n][:, cols], W2L[n][:, 1, :], start=False, stop=True)
                ins.then_inc(s_dn, 1)

            def step(x, m):
                at(turn, x, m, 0)
                at(up, x, m, 1)
                at(down, x, m, 3)

            pipeline(pe, step)

        @block.scalar
        def _(act):
            def high_rows(e, m):
                act.wait_ge(s_tr, e + 1)
                if late(e, 2):
                    act.wait_ge(s_up, e - 1)
                nc.scalar.activation(XTH[m % 2][:].rearrange("p k n -> p (k n)"), ps[:, B_T + m % 2, :], ACT.Copy).then_inc(s_xh, 1)

            def high_up(e, m):
                act.wait_ge(s_ew[m], loads(e, m, 80))
                if late(e, 2):
                    act.wait_ge(s_up, e - 1)
                nc.scalar.activation(WUH[m % 2][:].rearrange("p k n -> p (k n)"), WU[m][:].rearrange("p k n -> p (k n)"),
                                     ACT.Copy).then_inc(s_wh, 1)

            def high_down(e, m):
                if late(e, 2):
                    act.wait_ge(s_dn, e - 1)
                act.wait_ge(s_ew[m], loads(e, m, 80))
                nc.scalar.activation(W2H[m % 2][:].rearrange("p k n -> p (k n)"), W2[m][:].rearrange("p k n -> p (k n)"),
                                     ACT.Copy).then_inc(s_w2h, 1)

            def silu(e, m):
                act.wait_ge(s_up, e + 1)
                if late(e, 2):
                    act.wait_ge(s_h, e - 1)
                nc.scalar.activation(SG[m % 2][:].rearrange("p k n -> p (k n)"), ps[:, B_UP + 2 * (m % 2), :], ACT.Silu).then_inc(s_sg, 1)

            def high_hidden(e, m):
                act.wait_ge(s_h, e + 1)
                if late(e, 2):
                    act.wait_ge(s_dn, e - 1)
                nc.scalar.activation(HAH[m % 2][:], HA[m % 2][:], ACT.Copy)
                nc.scalar.activation(HBS[m % 2][0:TAIL, :], HB[m % 2][:], ACT.Copy).then_inc(s_hh, 1)

            def weighted(e, m):
                act.wait_ge(s_meta, e + 1)
                act.wait_ge(s_dn, e + 1)
                for st in range(2):
                    ins = nc.scalar.activation(O[m][:, st, :], ps[:, B_DN + m % 2, st * T:(st + 1) * T], ACT.Copy,
                                               scale=META[m][:, st, 0:1])
                ins.then_inc(s_o, 1)

            def step(x, m):
                at(high_up, x, m, 0)
                at(high_rows, x, m, 0)
                at(high_hidden, x, m, 2)
                at(weighted, x, m, 4)
                at(silu, x, m, 1)
                at(high_down, x, m, 1)

            pipeline(act, step)
            for n in range(PARTS):
                act.wait_ge(s_fin, n + 1)
                act.dma_start(out[n * PB:(n + 1) * PB].rearrange("b p t -> p b t"), X[:, n * PB:(n + 1) * PB, :]).then_inc(s_out, 16)
            act.wait_ge(s_out, 16 * PARTS)

        @block.vector
        def _(dve):
            def read_meta(e, m):
                dve.wait_ge(s_xb[m], loads(e, m, 16))
                nc.vector.tensor_copy(META0[m][:, :, 1:2], XB[m][:, :, ROW - 1:ROW])
                nc.vector.tensor_copy(META0[m][:, :, 0:1], XB[m][:, :, bass.ds(e + T, 1)]).then_inc(s_meta0, 1)

            def meta(e, m):
                dve.wait_ge(s_meta0, e + 1)
                if late(e, 4):
                    dve.wait_ge(s_acc[m % 2], 16 * (e - m) - 32 + 32 * (m // 2))
                nc.vector.tensor_copy(META[m][:], META0[m][:]).then_inc(s_meta, 1)

            def low_rows(e, m):
                dve.wait_ge(s_xh, e + 1)
                nc.vector.tensor_tensor(XTL[m % 2][:].rearrange("p k n -> p (k n)"), ps[:, B_T + m % 2, :],
                                        XTH[m % 2][:].rearrange("p k n -> p (k n)").bitcast(F32), ALU.subtract).then_inc(s_xl, 1)

            def low_up(e, m):
                dve.wait_ge(s_wh, e + 1)
                nc.vector.tensor_tensor(WUL[m % 2][:, :, POOLW:UPW], WU[m][:, :, POOLW:UPW],
                                        WUH[m % 2][:, :, POOLW:UPW].bitcast(F32), ALU.subtract).then_inc(s_wld, 1)

            def low_down(e, m):
                dve.wait_ge(s_w2h, e + 1)
                nc.vector.tensor_tensor(W2L[m % 2][:], W2[m][:], W2H[m % 2][:].bitcast(F32), ALU.subtract).then_inc(s_w2l, 1)

            def hidden(e, m):
                dve.wait_ge(s_sg, e + 1)
                b0 = B_UP + 2 * (m % 2)
                nc.vector.tensor_tensor(HA[m % 2][:], SG[m % 2][0:HEADW, 0, :], ps[0:HEADW, b0 + 1, 0:CAP], ALU.mult)
                nc.vector.tensor_tensor(HB[m % 2][:], SG[m % 2][0:TAIL, 1, :], ps[64:64 + TAIL, b0, CAP:2 * CAP],
                                        ALU.mult).then_inc(s_h, 1)

            def low_hidden(e, m):
                dve.wait_ge(s_hh, e + 1)
                nc.vector.tensor_tensor(HAL[m % 2][:], HA[m % 2][:], HAH[m % 2][:].bitcast(F32), ALU.subtract)
                nc.vector.tensor_tensor(HBS[m % 2][TAIL:2 * TAIL, :], HB[m % 2][:], HBS[m % 2][0:TAIL, :].bitcast(F32),
                                        ALU.subtract).then_inc(s_hl, 1)

            def step(x, m):
                at(low_down, x, m, 2)
                at(low_up, x, m, 0)
                at(low_rows, x, m, 0)
                at(read_meta, x, m, 0)
                at(low_hidden, x, m, 2)
                at(meta, x, m, 2)
                at(hidden, x, m, 1)

            pipeline(dve, step)
            dve.wait_ge(s_yeven, 16)
            half = slice(0, NB // 2)
            nc.vector.tensor_tensor(X[:, half, :], X[:, half, :], YS[:, 0, half, :], ALU.add).then_inc(s_even, 1)
            dve.wait_ge(s_even, 1)
            for n in range(PARTS):
                part = slice(n * PB, (n + 1) * PB)
                dve.wait_ge(s_yodd[n], 16)
                if n * PB >= NB // 2:
                    dve.wait_ge(s_even_rest, n - PARTS // 2 + 1)
                nc.vector.tensor_tensor(X[:, part, :], X[:, part, :], YS[:, 1, part, :], ALU.add).then_inc(s_fin, 1)


_INS = ["x", "cond_2048", "L0_cond_Wq", "L0_cond_Wo", "L0_ffn_gate_w", "L0_ffn_w1", "L0_ffn_w2", "L0_ffn_w3",
        "L0_ffn_sw1", "L0_ffn_sw2", "L0_ffn_sw3"]


def constants():
    import numpy as np

    p = np.arange(P)
    c = np.zeros((P, NCONST), np.float32)
    c[:, C_ID:C_ID + P] = np.eye(P)
    c[:, C_UP:C_UP + P] = p[:, None] < p[None, :]
    for k in range(2):
        for part in range(2):
            for h in range(2):
                c[4 * k + 2 * part + h, C_SEL + (2 * k + h) * P:C_SEL + (2 * k + h + 1) * P] = 1
    c[:, C_IOTA:C_IOTA + E] = np.arange(E)
    c[:, C_SPLIT] = -(p // 32 % 2)
    c[:, C_SPLIT + 1] = -(p // 16 % 2)
    c[:, C_TRASH] = TRASH + p
    c[:, C_DIAG:C_DIAG + NB] = p[:, None] % 32 == np.arange(NB)
    i = np.zeros((P, NB + 2), np.int32)
    i[:, :NB] = p[:, None] + P * np.arange(NB)
    i[:, NB:] = TOK + p[:, None] + P * np.arange(2)
    return c, i


def kernel(**inputs):
    import numpy as _np
    import concourse.bacc as _bacc
    from concourse import mybir as _mybir
    from concourse.bass_utils import run_bass_kernel_spmd as _run

    nc = _bacc.Bacc("TRN2", target_bir_lowering=False, num_devices=1)
    arrays, args = {}, []
    given = [_np.ascontiguousarray(inputs[name]) for name in _INS] + list(constants())
    for name, a in zip(_INS + ["constants", "token_numbers"], given):
        arrays[f"in_{name}"] = a
        args.append(nc.dram_tensor(f"in_{name}", a.shape, _mybir.dt.from_np(a.dtype), kind="ExternalInput").ap())
    out = nc.dram_tensor("out_0", (NB, D, T), _mybir.dt.float32, kind="ExternalOutput").ap()
    build(nc, *args, out)
    r = _run(nc, [arrays], core_ids=[0])
    return r.results[0]["out_0"]
```
